# Optimizing a Trainium2 kernel written in Bass

```python
import numpy as np
import jax
import jax.numpy as jnp

def _softmax(x, axis=-1):
    return jax.nn.softmax(x, axis=axis)

def _gelu(x):
    return jax.nn.gelu(x, approximate=True)

def _silu(x):
    return jax.nn.silu(x)

def _sigmoid(x):
    return jax.nn.sigmoid(x)

def _layernorm(x, axis=-1, eps=1e-05):
    m = jnp.mean(x, axis=axis, keepdims=True)
    v = jnp.var(x, axis=axis, keepdims=True)
    return (x - m) / jnp.sqrt(v + eps)

def _scatter_add(tgt, idx, src, axis=0):
    return tgt.at[idx].add(src)

def _segment_sum(src, seg, n):
    return jax.ops.segment_sum(src, seg, n)
kernel_name = 'mk_gnn_preln_d1_gnn_r8_afa90a'

def setup_inputs(seed: int=0):
    np.random.seed(seed)
    _w = jnp.asarray

    def _rec_inputs():
        import jax
        import jax.numpy as jnp
        _gk = jax.random.key(seed)
        x = -0.0005121 + 1.001 * jax.random.normal(jax.random.fold_in(_gk, 1), (6250, 64), jnp.float32)
        _s = jax.random.randint(jax.random.fold_in(_gk, 2), (100000,), 0, 6250, jnp.int32)
        _d = jax.random.randint(jax.random.fold_in(_gk, 3), (100000,), 0, 6250, jnp.int32)
        _loop = jnp.arange(6250, dtype=jnp.int32)
        src = jnp.concatenate([_s, _d, _loop])
        dst = jnp.concatenate([_d, _s, _loop])
        _o = jnp.argsort(dst, stable=True)
        src = src[_o]
        dst = dst[_o]
        edge_attr_32 = -9.77346e-05 + 0.999888 * jax.random.normal(jax.random.fold_in(_gk, 12), (206250, 32), jnp.float32)
        return (x, src, dst, edge_attr_32)
    x, src, dst, edge_attr_32 = _rec_inputs()

    def _L0_gnn_setup():
        import jax, jax.numpy as jnp
        import numpy as np
        N_NODES = 6250
        N_EDGES = 200000
        NODE_DIM = 64
        EDGE_DIM = 32
        UNITS = 64

        def _glorot(key, shape):
            fan_in, fan_out = (shape[0], shape[1])
            lim = jnp.sqrt(6.0 / (fan_in + fan_out))
            return jax.random.uniform(key, shape, jnp.float32, -lim, lim)
        key = jax.random.key(seed)
        ks = jax.random.split(key, 16)
        msg_in = 2 * NODE_DIM + EDGE_DIM
        upd_in = NODE_DIM + UNITS
        return {'node_features': jax.random.normal(ks[0], (N_NODES, NODE_DIM), jnp.float32), 'edge_features': jax.random.normal(ks[1], (N_EDGES, EDGE_DIM), jnp.float32), 'senders': jax.random.randint(ks[2], (N_EDGES,), 0, N_NODES, jnp.int32), 'receivers': jnp.sort(jax.random.randint(ks[3], (N_EDGES,), 0, N_NODES, jnp.int32)), 'W1': _glorot(ks[4], (msg_in, UNITS)), 'b1': jnp.zeros((UNITS,), jnp.float32), 'W2': _glorot(ks[5], (UNITS, UNITS)), 'b2': jnp.zeros((UNITS,), jnp.float32), 'Wa1': _glorot(ks[6], (msg_in, UNITS)), 'ba1': jnp.zeros((UNITS,), jnp.float32), 'Wa2': _glorot(ks[7], (UNITS, 1)), 'ba2': jnp.zeros((1,), jnp.float32), 'Wu1': _glorot(ks[8], (upd_in, UNITS)), 'bu1': jnp.zeros((UNITS,), jnp.float32), 'Wu2': _glorot(ks[9], (UNITS, UNITS)), 'bu2': jnp.zeros((UNITS,), jnp.float32)}
    _L0_gnn_all = _L0_gnn_setup()
    _L0_gnn_in = {k: v for k, v in _L0_gnn_all.items() if k in ('W1', 'b1', 'W2', 'b2', 'Wa1', 'ba1', 'Wa2', 'ba2', 'Wu1', 'bu1', 'Wu2', 'bu2')}
    del _L0_gnn_all
    return {'x': x, 'src': src, 'dst': dst, 'edge_attr_32': edge_attr_32, 'L0_gnn_W1': _L0_gnn_in['W1'], 'L0_gnn_b1': _L0_gnn_in['b1'], 'L0_gnn_W2': _L0_gnn_in['W2'], 'L0_gnn_b2': _L0_gnn_in['b2'], 'L0_gnn_Wa1': _L0_gnn_in['Wa1'], 'L0_gnn_ba1': _L0_gnn_in['ba1'], 'L0_gnn_Wa2': _L0_gnn_in['Wa2'], 'L0_gnn_ba2': _L0_gnn_in['ba2'], 'L0_gnn_Wu1': _L0_gnn_in['Wu1'], 'L0_gnn_bu1': _L0_gnn_in['bu1'], 'L0_gnn_Wu2': _L0_gnn_in['Wu2'], 'L0_gnn_bu2': _L0_gnn_in['bu2']}

def reference(x, src, dst, edge_attr_32, L0_gnn_W1, L0_gnn_b1, L0_gnn_W2, L0_gnn_b2, L0_gnn_Wa1, L0_gnn_ba1, L0_gnn_Wa2, L0_gnn_ba2, L0_gnn_Wu1, L0_gnn_bu1, L0_gnn_Wu2, L0_gnn_bu2):
    import jax
    import jax.numpy as jnp

    def _L0_gnn_ref(node_features, edge_features, senders, receivers, W1, b1, W2, b2, Wa1, ba1, Wa2, ba2, Wu1, bu1, Wu2, bu2):
        import jax, jax.numpy as jnp
        import numpy as np
        N_NODES = 6250
        N_EDGES = 200000
        NODE_DIM = 64
        EDGE_DIM = 32
        UNITS = 64

        def _glorot(key, shape):
            fan_in, fan_out = (shape[0], shape[1])
            lim = jnp.sqrt(6.0 / (fan_in + fan_out))
            return jax.random.uniform(key, shape, jnp.float32, -lim, lim)
        act = jax.nn.swish
        msg_in = jnp.concatenate([node_features[senders], node_features[receivers], edge_features], axis=-1)
        messages = act(msg_in @ W1 + b1) @ W2 + b2
        att_logits = act(msg_in @ Wa1 + ba1) @ Wa2 + ba2
        att = jax.nn.softmax(att_logits, axis=0)
        messages = messages * att
        aggregated = jax.ops.segment_sum(messages, receivers, num_segments=node_features.shape[0])
        upd_in = jnp.concatenate([node_features, aggregated], axis=-1)
        return act(upd_in @ Wu1 + bu1) @ Wu2 + bu2
    h = jnp.maximum(_layernorm(x, axis=-1), 0.0)
    x = x + _L0_gnn_ref(h, edge_attr_32, src, dst, L0_gnn_W1, L0_gnn_b1, L0_gnn_W2, L0_gnn_b2, L0_gnn_Wa1, L0_gnn_ba1, L0_gnn_Wa2, L0_gnn_ba2, L0_gnn_Wu1, L0_gnn_bu1, L0_gnn_Wu2, L0_gnn_bu2)
    return x

_drawn_inputs = setup_inputs


def setup_inputs(seed=0):
    import zlib

    import numpy as np

    out = dict(_drawn_inputs(seed))
    spreads = {'L0_gnn_b1': (0.0, 2.0),
     'L0_gnn_b2': (0.0, 2.0),
     'L0_gnn_ba1': (0.0, 0.8),
     'L0_gnn_bu1': (0.0, 0.1),
     'L0_gnn_bu2': (0.0, 0.1)}
    factors = {'edge_attr_32': 8.0,
     'L0_gnn_W1': 8.0,
     'L0_gnn_W2': 8.0,
     'L0_gnn_Wa1': 8.0,
     'L0_gnn_Wa2': 8.0}
    for name, (base, spread) in spreads.items():
        noise = np.random.default_rng([zlib.crc32(name.encode()), seed]).standard_normal(out[name].shape)
        drawn = base * np.exp(spread * noise) if base else spread * noise
        out[name] = jnp.asarray(drawn.astype(out[name].dtype))
    for name, factor in factors.items():
        out[name] = (out[name] * factor).astype(out[name].dtype)
    return out
```

```python
import concourse.bass as bass
from concourse import mybir
from contextlib import ExitStack

F32 = mybir.dt.float32
I32 = mybir.dt.int32
ALU = mybir.AluOpType
ACT = mybir.ActivationFunctionType
AX = mybir.AxisListType


def build(nc, x, src, dst, ef, W1, b1, W2, b2, Wa1, ba1, Wa2, ba2, Wu1, bu1, Wu2, bu2, out):
    N, D = x.shape
    E, DE = ef.shape
    U = W2.shape[0]
    P = 128
    H2 = 2 * U
    TG = 16
    GE = TG * P
    NG = -(-E // GE)
    LAST = NG - 1
    DUP = NG * GE - E
    TQ = 4
    NQ = TG // TQ
    WIN = P
    NT = -(-N // P)
    NP = NT * P
    LT = N - (NT - 1) * P
    NBT = 4
    NB = NT // NBT
    assert NT == NB * NBT + 1 and H2 == P and DE * TQ == P and NG % 2 == 1 and NB % 2 == 0
    EPS = 1e-5

    p_tab = nc.dram_tensor("p_tab", (N, H2), F32).ap()
    q_tab = nc.dram_tensor("q_tab", (N, H2), F32).ap()

    ctx = ExitStack()
    with ctx:
        def sb(name, shape, dt=F32):
            return ctx.enter_context(nc.sbuf_tensor(name, shape, dt))

        def sem(name):
            return ctx.enter_context(nc.semaphore(name))

        banks = [ctx.enter_context(nc.psum_tensor(f"bank{i}", [P, 512], F32)) for i in range(8)]

        ident = sb("ident", [P, P])
        iota = sb("iota", [P, P])
        ones = sb("ones", [P, P])
        minus_half = sb("minus_half", [P, NBT])
        mask = sb("mask", [P, TG])
        w_pq = sb("w_pq", [D + 1, 2 * H2])
        w_ed = sb("w_ed", [P, TQ, H2])
        wa2 = sb("wa2", [P, U])
        wa2h = sb("wa2h", [P, U])
        ba2c = sb("ba2c", [P, 1])
        w2e = sb("w2e", [U + 1, U])
        wu1h = sb("wu1h", [D + 1, U])
        wu1a = sb("wu1a", [U, U])
        wu2e = sb("wu2e", [U + 1, D])
        x_sb = sb("x_sb", [P, NT, D])
        hT = sb("hT", [D + 1, NP])
        stat = sb("stat", [P, 2, 4, NBT])
        first_i = sb("first_i", [1, NG], I32)
        first_f = sb("first_f", [1, NG])
        base_f = sb("base_f", [1, NG])
        base_i = sb("base_i", [1, NG], I32)
        base = sb("base", [P, NG])
        neg_max = sb("neg_max", [P, NG])
        rel_hi = sb("rel_hi", [P, NG])
        rel_lo = sb("rel_lo", [P, NG])
        src_i = sb("src_i", [P, 2, TG], I32)
        dst_i = sb("dst_i", [P, 2, TG], I32)
        ef_sb = sb("ef_sb", [P, 2, TG * DE])
        q_win = sb("q_win", [P, 2, H2])
        p_rows = sb("p_rows", [P, 2, TG * H2])
        rel = sb("rel", [P, 2, TG])
        hot = sb("hot", [P, 2, TG, WIN])
        hotT = sb("hotT", [P, TG * P])
        efT = sb("efT", [P, 2, TG * DE])
        z = sb("z", [P, TG, H2])
        th = sb("th", [P, TG, H2])
        s2 = sb("s2", [P, TG, H2])
        lg = sb("lg", [P, 2, TG])
        lgb = sb("lgb", [P, 2, TG])
        pmax = sb("pmax", [P, 2])
        gmax = sb("gmax", [1, 2])
        w = sb("w", [P, 2, TG])
        wm = sb("wm", [P, 2, TG])
        v = sb("v", [P, 2, TG, U + 1])
        part = sb("part", [U + 1, NG * WIN])
        flat = lambda t: t[:, :, :].rearrange("p t u -> p (t u)")
        hst = flat(z)[0:D + 1, 0:2 * NBT * P].rearrange("p (a n) -> p a n", a=2)
        xc = flat(s2)[:, 0:2 * NBT * D].rearrange("p (a t d) -> p a t d", a=2, t=NBT)
        hn = flat(s2)[:, 2 * NBT * D:4 * NBT * D].rearrange("p (a t d) -> p a t d", a=2, t=NBT)
        pq = flat(th)[:, 0:4 * NBT * H2].rearrange("p (a t u) -> p a t u", a=2, t=NBT)
        y = flat(p_rows)[:, 0:2 * NBT * D].rearrange("p (a t d) -> p a t d", a=2, t=NBT)
        acc = sb("acc", [U + 1, NP])
        top = sb("top", [P, 1])
        fac = sb("fac", [P, NG])
        zsum = sb("zsum", [U + 1, 1])
        zall = sb("zall", [U, 1])
        rz = sb("rz", [U, 1])
        agg = z[:, :, :].rearrange("p t u -> p (t u)")[0:U, 0:1024].rearrange("p (a n) -> p a n", a=2)
        thu = th[:, :, :].rearrange("p t u -> p (t u)")[0:U, 0:1024].rearrange("p (a n) -> p a n", a=2)
        su = sb("su", [U + 1, 2, 512])

        ps_efT = banks[0]
        ps_hotT = banks[1:3]
        ps_z = banks[3:5]
        ps_part = banks[5]
        ps_maxT = banks[6]
        ps_maxB = banks[7]
        ps_hT = banks[0]
        ps_pq = banks[1:3]
        ps_base = banks[7]
        ps_agg = banks[0:2]
        ps_u = banks[2:4]
        ps_y = banks[4:6]
        ps_zall = banks[6]

        w_ld, w_ld2, x_ld, first_ld = sem("w_ld"), sem("w_ld2"), sem("x_ld"), sem("first_ld")
        zeroed, ident_ok, iota_ok, const_ok = sem("zeroed"), sem("ident_ok"), sem("iota_ok"), sem("const_ok")
        halved, dstep, w_ed_zero, rstd_ok = sem("halved"), sem("dstep"), sem("w_ed_zero"), sem("rstd_ok")
        var_ok = sem("var_ok")
        base_ok, baseB_done, baseB_ok = sem("base_ok"), sem("baseB_done"), sem("baseB_ok")
        hn_ok, hT_done, hst_ok, hT_ok, pq_done, pq_ok = (sem(n) for n in ("hn_ok", "hT_done", "hst_ok", "hT_ok", "pq_done", "pq_ok"))
        p_st = [sem("p_st0"), sem("p_st1")]
        ld = [sem("ld0"), sem("ld1")]
        win_ld = [sem("win_ld0"), sem("win_ld1")]
        gath = [[sem(f"gath{a}{q}") for q in range(NQ)] for a in range(2)]
        rel_ok, hot_ok = sem("rel_ok"), sem("hot_ok")
        efT_done, efT_ok, hotT_done, hotT_ok = (sem(n) for n in ("efT_done", "efT_ok", "hotT_done", "hotT_ok"))
        z_done, z_ok, th_ok, s_ok, prod_ok, lgq_ok = (sem(n) for n in ("z_done", "z_ok", "th_ok", "s_ok", "prod_ok", "lgq_ok"))
        lg_ok, pmax_ok, maxT_done, gmax_ok, maxB_done, negm_ok = (sem(n) for n in ("lg_ok", "pmax_ok", "maxT_done", "gmax_ok", "maxB_done", "negm_ok"))
        w_ok, wm_ok, v_ok, part_done, part_ok = (sem(n) for n in ("w_ok", "wm_ok", "v_ok", "part_done", "part_ok"))
        acc_zero, top_ok, fac_ok, merged, zsum_ok, zall_done, zall_ok, rz_ok = (sem(n) for n in ("acc_zero", "top_ok", "fac_ok", "merged", "zsum_ok", "zall_done", "zall_ok", "rz_ok"))
        agg_done, agg_ok, u_done, thu_ok, su_ok, y_done, y_ok = (sem(n) for n in ("agg_done", "agg_ok", "u_done", "thu_ok", "su_ok", "y_done", "y_ok"))
        pe_turn, pool_turn = sem("pe_turn"), sem("pool_turn")
        out_st = [sem("out_st0"), sem("out_st1")]

        x_t = x[0:(NT - 1) * P, :].rearrange("(t p) d -> p t d", p=P)
        p_t = p_tab[0:(NT - 1) * P, :].rearrange("(t p) d -> p t d", p=P)
        q_t = q_tab[0:(NT - 1) * P, :].rearrange("(t p) d -> p t d", p=P)
        out_t = out[0:(NT - 1) * P, :].rearrange("(t p) d -> p t d", p=P)

        def wait(eng, s, n):
            if not (isinstance(n, int) and n <= 0):
                eng.wait_ge(s, n)

        def groups(eng, body):
            body(0, 0)
            body(1, 1)
            with eng.Fori(1, LAST // 2) as pair:
                body(pair * 2, 0)
                body(pair * 2 + 1, 1)
            body(LAST, 0)

        def batches(eng, body):
            body(0, 0, NBT)
            body(1, 1, NBT)
            with eng.Fori(1, NB // 2) as pair:
                body(pair * 2, 0, NBT)
                body(pair * 2 + 1, 1, NBT)
            body(NB, 0, 1)

        def edge0(g):
            return E - GE if isinstance(g, int) and g == LAST else g * GE

        def per(a, g, n):
            return (g - a) * (n // 2) + n

        block = ctx.enter_context(nc.Block())

        @block.sync
        def _(sp):
            sp.dma_start(x_sb[:, 0:NT - 1, :], x_t).then_inc(x_ld, 16)
            sp.wait_ge(zeroed, 1)
            sp.dma_start(x_sb[0:LT, NT - 1, :], x[(NT - 1) * P:N, :]).then_inc(x_ld, 16)
            sp.dma_start(w_pq[0:D, 0:U], W1[0:D, :]).then_inc(w_ld, 16)
            sp.dma_start(w_pq[0:D, U:H2], Wa1[0:D, :]).then_inc(w_ld, 16)
            sp.dma_start(w_pq[0:D, H2:H2 + U], W1[D:2 * D, :]).then_inc(w_ld, 16)
            sp.dma_start(w_pq[0:D, H2 + U:2 * H2], Wa1[D:2 * D, :]).then_inc(w_ld, 16)
            sp.dma_start(w_pq[D:D + 1, H2:H2 + U], b1[None, :]).then_inc(w_ld, 16)
            sp.dma_start(w_pq[D:D + 1, H2 + U:2 * H2], ba1[None, :]).then_inc(w_ld, 16)
            with nc.allow_non_contiguous_dma(reason="one dst of each group"):
                sp.dma_start(first_i[:, 0:LAST], dst[0:LAST * GE].rearrange("(a g e) -> a g e", a=1, e=GE)[:, :, 0]).then_inc(first_ld, 16)
            sp.dma_start(first_i[:, LAST:NG], dst[E - GE:E - GE + 1][None, :]).then_inc(first_ld, 16)
            sp.wait_ge(w_ed_zero, 1)
            for t in range(TQ):
                sp.dma_start(w_ed[t * DE:(t + 1) * DE, t, 0:U], W1[2 * D:2 * D + DE, :]).then_inc(w_ld2, 16)
                sp.dma_start(w_ed[t * DE:(t + 1) * DE, t, U:H2], Wa1[2 * D:2 * D + DE, :]).then_inc(w_ld2, 16)

            def store_tables(b, a, nt):
                sp.wait_ge(pq_ok, 2 * b + 2 if nt > 1 else 2 * b + 1)
                if nt > 1:
                    sp.dma_start(p_t[:, bass.ds(b * NBT, NBT), :], pq[:, a, :, 0:H2]).then_inc(p_st[a], 16)
                    sp.dma_start(q_t[:, bass.ds(b * NBT, NBT), :], pq[:, a, :, H2:2 * H2]).then_inc(p_st[a], 16)
                else:
                    sp.dma_start(p_tab[(NT - 1) * P:N, :], pq[0:LT, a, 0, 0:H2]).then_inc(p_st[a], 16)
                    sp.dma_start(q_tab[(NT - 1) * P:N, :], pq[0:LT, a, 0, H2:2 * H2]).then_inc(p_st[a], 16)
            batches(sp, store_tables)

            def load_group(g, a):
                wait(sp, z_ok, (g - 1) * NQ)
                wait(sp, rel_ok, g - 1)
                wait(sp, efT_done, g - 1)
                e0 = edge0(g)
                sp.dma_start(src_i[:, a, :], src[bass.ds(e0, GE)].rearrange("(p t) -> p t", t=TG)).then_inc(ld[a], 16)
                sp.dma_start(dst_i[:, a, :], dst[bass.ds(e0, GE)].rearrange("(p t) -> p t", t=TG)).then_inc(ld[a], 16)
                sp.dma_start(ef_sb[:, a, :], ef[bass.ds(e0, GE), :].rearrange("(p t) f -> p (t f)", t=TG)).then_inc(ld[a], 16)
            groups(sp, load_group)

            def store_out(b, a, nt):
                sp.wait_ge(y_ok, b + 1)
                if nt > 1:
                    sp.dma_start(out_t[:, bass.ds(b * NBT, NBT), :], y[:, a, :, :]).then_inc(out_st[a], 16)
                else:
                    sp.dma_start(out[(NT - 1) * P:N, :], y[0:LT, a, 0, :]).then_inc(out_st[a], 16)
            batches(sp, store_out)
            sp.wait_ge(out_st[0], 16 * (NB // 2 + 1))
            sp.wait_ge(out_st[1], 16 * (NB // 2))

        @block.gpsimd
        def _(pool):
            nc.gpsimd.memset(x_sb[:, NT - 1, :], 0.0).then_inc(zeroed, 1)
            nc.gpsimd.memset(ident[:], 0.0).then_inc(zeroed, 1)
            nc.gpsimd.memset(ones[:], 1.0).then_inc(const_ok, 1)
            nc.gpsimd.iota(iota[:], [[1, P]], base=0, channel_multiplier=0, allow_small_or_imprecise_dtypes=True).then_inc(iota_ok, 1)
            nc.gpsimd.memset(mask[:], 0.0).then_inc(zeroed, 1)
            pool.wait_ge(zeroed, 3)
            nc.gpsimd.affine_select(out=ident[:], in_=ident[:], compare_op=ALU.not_equal, fill=1.0,
                                    base=0, pattern=[[-1, P]], channel_multiplier=1).then_inc(ident_ok, 1)
            nc.gpsimd.affine_select(out=mask[:], in_=mask[:], compare_op=ALU.is_gt, fill=1.0,
                                    base=DUP, pattern=[[-1, TG]], channel_multiplier=-TG).then_inc(const_ok, 1)
            nc.gpsimd.memset(acc[:], 0.0).then_inc(acc_zero, 1)
            nc.gpsimd.memset(minus_half[:], -0.5).then_inc(zeroed, 1)
            pool.wait_ge(zeroed, 4)

            def rstd(b, a, nt):
                pool.wait_ge(var_ok, b + 1)
                nc.gpsimd.tensor_tensor(stat[:, a, 3, 0:nt], stat[:, a, 0, 0:nt], minus_half[:, 0:nt], ALU.pow).then_inc(rstd_ok, 1)
            batches(pool, rstd)
            pool.wait_ge(p_st[0], 32 * (NB // 2 + 1))
            pool.wait_ge(p_st[1], 32 * (NB // 2))

            def gather(g, a):
                pool.wait_ge(ld[a], per(a, g, 48))
                for q in range(NQ):
                    wait(pool, z_ok, (g - 2) * NQ + q + 1)
                    pool.sem_inc(pool_turn, 1)
                    for t in range(q * TQ, (q + 1) * TQ):
                        pool.indirect_dma_start(p_rows[:, a, t * H2:(t + 1) * H2], None, p_tab,
                                                bass.IndirectOffsetOnAxis(src_i[:, a, t:t + 1], 0)).then_inc(gath[a][q], 16)
            groups(pool, gather)

        @block.scalar
        def _(act):
            act.dma_start(wa2[:], Wa2.rearrange("a b -> b a").broadcast_to([P, U])).then_inc(w_ld2, 16)
            act.dma_start(ba2c[:], ba2[None, :].broadcast_to([P, 1])).then_inc(w_ld2, 16)
            act.dma_start(w2e[0:U, :], W2).then_inc(w_ld2, 16)
            act.dma_start(w2e[U:U + 1, :], b2[None, :]).then_inc(w_ld2, 16)
            act.dma_start(wu1h[0:D, :], Wu1[0:D, :]).then_inc(w_ld2, 16)
            act.dma_start(wu1h[D:D + 1, :], bu1[None, :]).then_inc(w_ld2, 16)
            act.dma_start(wu1a[:], Wu1[D:D + U, :]).then_inc(w_ld2, 16)
            act.dma_start(wu2e[0:U, :], Wu2).then_inc(w_ld2, 16)
            act.dma_start(wu2e[U:U + 1, :], bu2[None, :]).then_inc(w_ld2, 16)

            def node_rows(b, a, nt):
                n = nt * P
                act.wait_ge(hT_done, b + 1)
                wait(act, pq_done, 2 * (b - 1))
                nc.scalar.activation(hst[0:D, a, 0:n], ps_hT[0:D, 0:n], ACT.Relu).then_inc(hst_ok, 1)
                nc.scalar.activation(hT[0:D, bass.ds(b * NBT * P, n)], ps_hT[0:D, 0:n], ACT.Relu).then_inc(hT_ok, 1)
            batches(act, node_rows)
            act.wait_ge(p_st[0], 32 * (NB // 2 + 1))
            act.wait_ge(p_st[1], 32 * (NB // 2))
            act.wait_ge(base_ok, 1)

            def group(g, a):
                wait(act, z_done, (g - 1) * NQ)
                node = act.value_load(base_i[0:1, bass.ds(g, 1)], min_val=0, max_val=N - WIN)
                act.dma_start(q_win[:, a, :], q_tab[bass.ds(node, WIN), :]).then_inc(win_ld[a], 16)
                act.wait_ge(efT_done, g + 1)
                nc.scalar.copy(efT[:, a, :], ps_efT[:]).then_inc(efT_ok, 1)
                for q in range(NQ):
                    act.wait_ge(hotT_done, g * NQ + q + 1)
                    wait(act, z_done, (g - 1) * NQ + q + 1)
                    nc.scalar.copy(hotT[:, q * 512:(q + 1) * 512], ps_hotT[q % 2][:]).then_inc(hotT_ok, 1)
                for q in range(NQ):
                    ts = slice(q * TQ, (q + 1) * TQ)
                    act.wait_ge(z_ok, g * NQ + q + 1)
                    nc.scalar.activation(th[:, ts, :], z[:, ts, :], ACT.Tanh, scale=0.5).then_inc(th_ok, 1)
                act.wait_ge(negm_ok, g + 1)
                nc.scalar.activation(w[:, a, :], lgb[:, a, :], ACT.Exp, bias=neg_max[:, bass.ds(g, 1)]).then_inc(w_ok, 1)
            groups(act, group)
            act.wait_ge(top_ok, 1)
            nc.scalar.activation(fac[:], neg_max[:], ACT.Exp, scale=-1.0, bias=top[:]).then_inc(fac_ok, 1)
            act.wait_ge(rz_ok, 1)

            def update(b, a, nt):
                n = nt * P
                act.wait_ge(agg_done, b + 1)
                wait(act, u_done, b - 1)
                nc.scalar.activation(agg[:, a, 0:n], ps_agg[a][0:U, 0:n], ACT.Copy, scale=rz[:]).then_inc(agg_ok, 1)
                act.wait_ge(u_done, b + 1)
                wait(act, su_ok, b - 1)
                nc.scalar.activation(thu[:, a, 0:n], ps_u[a][0:U, 0:n], ACT.Tanh, scale=0.5).then_inc(thu_ok, 1)
            batches(act, update)

        @block.tensor
        def _(pe):
            pe.wait_ge(ident_ok, 1)
            pe.wait_ge(const_ok, 5)
            pe.wait_ge(w_ld, 96)
            pe.wait_ge(halved, 1)

            def node_rows(b, a, nt):
                pe.wait_ge(hn_ok, b + 1)
                wait(pe, hT_ok, b)
                pe.sem_inc(pe_turn, 1)
                for t in range(nt):
                    last = nc.tensor.transpose(ps_hT[0:D, t * P:(t + 1) * P], hn[:, a, t, :], ident[:])
                last.then_inc(hT_done, 1)
                pe.wait_ge(hst_ok, b + 1)
                for k in range(-(-nt // 2)):
                    wait(pe, pq_ok, 2 * (b - 1) + k + 1)
                    for t in range(2 * k, min(2 * k + 2, nt)):
                        last = nc.tensor.matmul(ps_pq[k][:, (t % 2) * 2 * H2:(t % 2 + 1) * 2 * H2], hst[:, a, t * P:(t + 1) * P], w_pq[:],
                                                start=True, stop=True)
                    last.then_inc(pq_done, 1)
            batches(pe, node_rows)
            pe.wait_ge(base_ok, 1)
            nc.tensor.matmul(ps_base[:, 0:NG], ones[0:1, :], base_f[:], start=True, stop=True).then_inc(baseB_done, 1)
            pe.wait_ge(baseB_ok, 1)
            pe.wait_ge(hT_ok, NB + 1)
            pe.wait_ge(pq_ok, 2 * NB + 1)
            pe.wait_ge(w_ld2, 16 * (2 * TQ + 9))

            def group(g, a):
                pe.wait_ge(ld[a], per(a, g, 48))
                wait(pe, efT_ok, g)
                for q in range(NQ):
                    last = nc.tensor.transpose(ps_efT[:, q * P:(q + 1) * P], ef_sb[:, a, q * P:(q + 1) * P], ident[:])
                last.then_inc(efT_done, 1)
                pe.wait_ge(hot_ok, g + 1)
                for q in range(NQ):
                    wait(pe, hotT_ok, g * NQ + q - 1)
                    for t in range(TQ):
                        last = nc.tensor.transpose(ps_hotT[q % 2][:, t * P:(t + 1) * P], hot[:, a, q * TQ + t, :], ident[:])
                    last.then_inc(hotT_done, 1)
                pe.wait_ge(efT_ok, g + 1)
                pe.wait_ge(win_ld[a], per(a, g, 16))
                for q in range(NQ):
                    wait(pe, z_ok, g * NQ + q - 1)
                    pe.wait_ge(hotT_ok, g * NQ + q + 1)
                    nc.tensor.matmul(ps_z[q % 2][:], efT[:, a, q * P:(q + 1) * P], w_ed[:].rearrange("p t u -> p (t u)"),
                                     start=True, stop=False, skip_group_check=True)
                    for t in range(TQ):
                        last = nc.tensor.matmul(ps_z[q % 2][:, t * H2:(t + 1) * H2], hotT[:, (q * TQ + t) * P:(q * TQ + t + 1) * P], q_win[:, a, :],
                                                start=False, stop=(t == TQ - 1), skip_group_check=True)
                    last.then_inc(z_done, 1)
                pe.wait_ge(pmax_ok, g + 1)
                nc.tensor.transpose(ps_maxT[0:1, 0:P], pmax[:, a:a + 1], ident[:]).then_inc(maxT_done, 1)
                pe.wait_ge(gmax_ok, g + 1)
                nc.tensor.matmul(ps_maxB[:, 0:1], ones[0:1, :], gmax[:, a:a + 1], start=True, stop=True).then_inc(maxB_done, 1)
                pe.wait_ge(v_ok, g + 1)
                wait(pe, part_ok, g)
                for t in range(TG):
                    last = nc.tensor.matmul(ps_part[0:U + 1, 0:WIN], v[:, a, t, :], hot[:, a, t, :], start=(t == 0), stop=(t == TG - 1))
                last.then_inc(part_done, 1)
            groups(pe, group)
            pe.wait_ge(zsum_ok, 1)
            pe.wait_ge(part_ok, NG)
            nc.tensor.matmul(ps_zall[0:U, 0:1], ones[U:U + 1, 0:U], zsum[U:U + 1, :], start=True, stop=True).then_inc(zall_done, 1)

            def update(b, a, nt):
                n = nt * P
                wait(pe, agg_ok, b - 1)
                nc.tensor.matmul(ps_agg[a][0:U, 0:n], w2e[:], acc[:, bass.ds(b * NBT * P, n)], start=True, stop=True).then_inc(agg_done, 1)
                wait(pe, su_ok, b - 1)
                nc.tensor.matmul(ps_u[a][0:U, 0:n], wu1h[:], hT[:, bass.ds(b * NBT * P, n)], start=True, stop=False)
                pe.wait_ge(agg_ok, b + 1)
                pe.sem_inc(pe_turn, 1)
                nc.tensor.matmul(ps_u[a][0:U, 0:n], wu1a[:], agg[:, a, 0:n], start=False, stop=True).then_inc(u_done, 1)
                pe.wait_ge(su_ok, b + 1)
                wait(pe, y_ok, b - 1)
                for t in range(nt):
                    last = nc.tensor.matmul(ps_y[a][:, t * D:(t + 1) * D], su[:, a, t * P:(t + 1) * P], wu2e[:], start=True, stop=True)
                last.then_inc(y_done, 1)
            batches(pe, update)

        @block.vector
        def _(dve):
            steps = [0]

            def chain(ins):
                steps[0] += 1
                ins.then_inc(dstep, 1)
                dve.wait_ge(dstep, steps[0])

            nc.vector.memset(w_ed[:], 0.0).then_inc(w_ed_zero, 1)
            nc.vector.memset(hst[D:D + 1, :, :], 1.0).then_inc(const_ok, 1)
            nc.vector.memset(hT[D:D + 1, :], 1.0).then_inc(const_ok, 1)
            nc.vector.memset(su[U:U + 1, :, :], 1.0).then_inc(const_ok, 1)
            nc.vector.memset(w_pq[D:D + 1, 0:H2], 0.0).then_inc(halved, 1)
            dve.wait_ge(first_ld, 32)
            chain(nc.vector.tensor_copy(first_f[:], first_i[:]))
            chain(nc.vector.tensor_scalar(base_f[:], first_f[:], float(N - WIN), None, ALU.min))
            nc.vector.tensor_copy(base_i[:], base_f[:]).then_inc(base_ok, 1)
            dve.wait_ge(x_ld, 32)

            def node_rows(b, a, nt):
                wait(dve, hT_done, b - 1)
                if nt > 1:
                    xs = x_sb[:, bass.ds(b * NBT, nt), :]
                else:
                    xs = x_sb[:, NT - 1:NT, :]
                st = [stat[:, a, i, 0:nt] for i in range(4)]
                big = [P, nt, D]
                n0 = b * 5 + 2
                k = [0]

                def link(ins):
                    k[0] += 1
                    ins.then_inc(dstep, 1)
                    dve.wait_ge(dstep, n0 + k[0])
                link(nc.vector.tensor_reduce(st[0], xs, AX.X, ALU.add))
                link(nc.vector.tensor_scalar(st[1], st[0], 1.0 / D, None, ALU.mult))
                link(nc.vector.tensor_tensor(xc[:, a, 0:nt, :], xs, st[1].unsqueeze(2).broadcast_to(big), ALU.subtract))
                link(nc.vector.tensor_tensor(hn[:, a, 0:nt, :], xc[:, a, 0:nt, :], xc[:, a, 0:nt, :], ALU.mult))
                link(nc.vector.tensor_reduce(st[2], hn[:, a, 0:nt, :], AX.X, ALU.add))
                nc.vector.tensor_scalar(st[0], st[2], 1.0 / D, EPS, ALU.mult, ALU.add).then_inc(var_ok, 1)
                dve.wait_ge(rstd_ok, b + 1)
                nc.vector.tensor_tensor(hn[:, a, 0:nt, :], xc[:, a, 0:nt, :], st[3].unsqueeze(2).broadcast_to(big), ALU.mult).then_inc(hn_ok, 1)
                for j in range(-(-nt // 2)):
                    m = min(2, nt - 2 * j)
                    dve.wait_ge(pq_done, 2 * b + j + 1)
                    if j == 0:
                        wait(dve, p_st[a], 16 * (b - a))
                    nc.vector.tensor_copy(pq[:, a, 2 * j:2 * j + m, :], ps_pq[j][:, 0:m * 2 * H2]).then_inc(pq_ok, 1)
            batches(dve, node_rows)
            dve.wait_ge(baseB_done, 1)
            nc.vector.tensor_copy(base[:], ps_base[:, 0:NG]).then_inc(baseB_ok, 1)
            dve.wait_ge(w_ld2, 16 * (2 * TQ + 9))
            nc.vector.tensor_scalar(wa2h[:], wa2[:], 0.5, None, ALU.mult).then_inc(halved, 1)
            nc.vector.tensor_scalar(w2e[0:U, :], w2e[0:U, :], 0.5, None, ALU.mult).then_inc(halved, 1)
            nc.vector.tensor_scalar(wu2e[0:U, :], wu2e[0:U, :], 0.5, None, ALU.mult).then_inc(halved, 1)
            dve.wait_ge(halved, 4)
            dve.wait_ge(iota_ok, 1)
            dve.wait_ge(baseB_ok, 1)

            def group(g, a):
                dve.wait_ge(ld[a], per(a, g, 48))
                nc.vector.tensor_scalar(rel[:, a, :], dst_i[:, a, :], base[:, bass.ds(g, 1)], None, ALU.subtract).then_inc(rel_ok, 1)
                dve.wait_ge(rel_ok, g + 1)
                nc.vector.tensor_tensor(hot[:, a, :, :], iota[:].unsqueeze(1).broadcast_to([P, TG, WIN]),
                                        rel[:, a, :].unsqueeze(2).broadcast_to([P, TG, WIN]), ALU.is_equal).then_inc(hot_ok, 1)
                nc.vector.tensor_reduce(rel_hi[:, bass.ds(g, 1)], rel[:, a, :], AX.X, ALU.max)
                nc.vector.tensor_reduce(rel_lo[:, bass.ds(g, 1)], rel[:, a, :], AX.X, ALU.min)
                for q in range(NQ):
                    ts = slice(q * TQ, (q + 1) * TQ)
                    dve.wait_ge(z_done, g * NQ + q + 1)
                    dve.wait_ge(gath[a][q], per(a, g, 16 * TQ))
                    nc.vector.tensor_tensor(z[:, ts, :], ps_z[q % 2][:].rearrange("p (t u) -> p t u", t=TQ),
                                            p_rows[:, a, q * 512:(q + 1) * 512].rearrange("p (t u) -> p t u", t=TQ), ALU.add).then_inc(z_ok, 1)
                    dve.wait_ge(th_ok, g * NQ + q + 1)
                    nc.vector.scalar_tensor_tensor(s2[:, ts, :], th[:, ts, :], 1.0, z[:, ts, :], ALU.add, ALU.mult).then_inc(s_ok, 1)
                    dve.wait_ge(s_ok, g * NQ + q + 1)
                    nc.vector.tensor_tensor(z[:, ts, U:H2], s2[:, ts, U:H2], wa2h[:].unsqueeze(1).broadcast_to([P, TQ, U]), ALU.mult).then_inc(prod_ok, 1)
                    dve.wait_ge(prod_ok, g * NQ + q + 1)
                    nc.vector.tensor_reduce(lg[:, a, ts], z[:, ts, U:H2], AX.X, ALU.add).then_inc(lgq_ok, 1)
                dve.wait_ge(lgq_ok, (g + 1) * NQ)
                nc.vector.tensor_scalar(lgb[:, a, :], lg[:, a, :], ba2c[:], None, ALU.add).then_inc(lg_ok, 1)
                dve.wait_ge(lg_ok, g + 1)
                nc.vector.tensor_reduce(pmax[:, a:a + 1], lgb[:, a, :], AX.X, ALU.max).then_inc(pmax_ok, 1)
                dve.wait_ge(maxT_done, g + 1)
                nc.vector.tensor_reduce(gmax[:, a:a + 1], ps_maxT[0:1, 0:P], AX.X, ALU.max).then_inc(gmax_ok, 1)
                dve.wait_ge(maxB_done, g + 1)
                nc.vector.tensor_scalar(neg_max[:, bass.ds(g, 1)], ps_maxB[:, 0:1], -1.0, None, ALU.mult).then_inc(negm_ok, 1)
                dve.wait_ge(w_ok, g + 1)
                ww = w
                if isinstance(g, int) and g == LAST:
                    nc.vector.tensor_tensor(wm[:, a, :], w[:, a, :], mask[:], ALU.mult).then_inc(wm_ok, 1)
                    dve.wait_ge(wm_ok, 1)
                    ww = wm
                nc.vector.tensor_copy(v[:, a, :, U:U + 1], ww[:, a, :].unsqueeze(2))
                nc.vector.tensor_tensor(v[:, a, :, 0:U], s2[:, :, 0:U], ww[:, a, :].unsqueeze(2).broadcast_to([P, TG, U]), ALU.mult).then_inc(v_ok, 1)
                dve.wait_ge(part_done, g + 1)
                nc.vector.tensor_copy(part[:, bass.ds(g * WIN, WIN)], ps_part[0:U + 1, 0:WIN]).then_inc(part_ok, 1)
            groups(dve, group)
            nc.vector.tensor_reduce(top[:], neg_max[:], AX.X, ALU.min).then_inc(top_ok, 1)
            dve.wait_ge(fac_ok, 1)
            dve.wait_ge(part_ok, NG)
            dve.wait_ge(acc_zero, 1)

            def merge(g):
                node = dve.value_load(base_i[0:1, bass.ds(g, 1)], min_val=0, max_val=N - WIN)
                wait(dve, merged, g)
                nc.vector.scalar_tensor_tensor(acc[:, bass.ds(node, WIN)], part[:, bass.ds(g * WIN, WIN)], fac[0:U + 1, bass.ds(g, 1)],
                                               acc[:, bass.ds(node, WIN)], ALU.mult, ALU.add).then_inc(merged, 1)
            merge(0)
            with dve.Fori(1, NG) as g:
                merge(g)
            dve.wait_ge(merged, NG)
            nc.vector.tensor_reduce(zsum[U:U + 1, :], acc[U:U + 1, :], AX.X, ALU.add).then_inc(zsum_ok, 1)
            dve.wait_ge(zall_done, 1)
            nc.vector.tensor_copy(zall[:], ps_zall[0:U, 0:1]).then_inc(zall_ok, 1)
            dve.wait_ge(zall_ok, 1)
            nc.vector.reciprocal(rz[:], zall[:]).then_inc(rz_ok, 1)

            def update(b, a, nt):
                n = nt * P
                dve.wait_ge(thu_ok, b + 1)
                wait(dve, y_done, b - 1)
                nc.vector.scalar_tensor_tensor(su[0:U, a, 0:n], thu[:, a, 0:n], 1.0, ps_u[a][0:U, 0:n], ALU.add, ALU.mult).then_inc(su_ok, 1)
                dve.wait_ge(y_done, b + 1)
                wait(dve, out_st[a], 8 * (b - a))
                xs = x_sb[:, bass.ds(b * NBT, nt), :]
                nc.vector.tensor_tensor(y[:, a, 0:nt, :], ps_y[a][:, 0:nt * D].rearrange("p (t d) -> p t d", t=nt), xs, ALU.add).then_inc(y_ok, 1)
            batches(dve, update)


_INS = ["x", "src", "dst", "edge_attr_32"] + ["L0_gnn_" + n for n in
        ("W1", "b1", "W2", "b2", "Wa1", "ba1", "Wa2", "ba2", "Wu1", "bu1", "Wu2", "bu2")]


def kernel(**inputs):
    import numpy as np
    import concourse.bacc as bacc
    from concourse.bass_utils import run_bass_kernel_spmd

    nc = bacc.Bacc("TRN2", target_bir_lowering=False, num_devices=1)
    arrays, args = {}, []
    for name in _INS:
        a = np.ascontiguousarray(inputs[name])
        arrays[name] = a
        args.append(nc.dram_tensor(name, a.shape, mybir.dt.from_np(a.dtype), kind="ExternalInput").ap())
    args.append(nc.dram_tensor("out", inputs["x"].shape, F32, kind="ExternalOutput").ap())
    build(nc, *args)
    r = run_bass_kernel_spmd(nc, [arrays], core_ids=[0])
    return r.results[0]["out"]
```

```python
import concourse.bass as bass
from concourse import mybir
from contextlib import ExitStack

F32 = mybir.dt.float32
BF16 = mybir.dt.bfloat16
I32 = mybir.dt.int32
ALU = mybir.AluOpType
ACT = mybir.ActivationFunctionType
AX = mybir.AxisListType


def build(nc, x, src, dst, ef, W1, b1, W2, b2, Wa1, ba1, Wa2, ba2, Wu1, bu1, Wu2, bu2, out):
    N, D = x.shape
    E, DE = ef.shape
    U = W2.shape[0]
    P = 128
    H2 = 2 * U
    TG = 20
    GE = TG * P
    NG = -(-E // GE)
    LAST = NG - 1
    TQ = 4
    NQ = TG // TQ
    TL = -(-(E - LAST * GE) // (TQ * P)) * TQ
    DUP = LAST * GE + TL * P - E
    WIN = P - DE
    NT = -(-N // P)
    NP = NT * P
    LT = N - (NT - 1) * P
    NBT = 4
    NB = NT // NBT
    assert NT == NB * NBT + 1 and H2 == P and DE * TQ == P and NG % 2 == 1 and NB % 2 == 0
    HALVES = [(0, 6 * NBT), (6 * NBT, NT)]
    EPS = 1e-5
    LOW = -3.0e38

    p_tab = nc.dram_tensor("p_tab", (N, H2), F32).ap()
    q_tab = nc.dram_tensor("q_tab", (N, H2), F32).ap()

    ctx = ExitStack()
    with ctx:
        def sb(name, shape, dt=F32):
            return ctx.enter_context(nc.sbuf_tensor(name, shape, dt))

        def sem(name):
            return ctx.enter_context(nc.semaphore(name))

        def flat(t):
            return t[:].rearrange("p a b -> p (a b)")

        ident = sb("ident", [P, P])
        iota = sb("iota", [P, P])
        row_no = sb("row_no", [P, 1])
        ones = sb("ones", [P, P])
        tile0 = sb("tile0", [P, NT])
        mask = sb("mask", [P, TL])
        sel = sb("sel", [TG, TG, P], BF16)
        w_p = sb("w_p", [D, H2])
        w_q = sb("w_q", [D + 1, H2])
        wa2 = sb("wa2", [P, U])
        wa2h = sb("wa2h", [P, U])
        ba2c = sb("ba2c", [P, 1])
        w2e = sb("w2e", [U + 1, U])
        wu1h = sb("wu1h", [D + 1, U])
        wu1a = sb("wu1a", [U, U])
        wu2e = sb("wu2e", [U + 1, D])
        x_sb = sb("x_sb", [P, NT, D])
        hT = sb("hT", [D + 1, NP])
        stat = sb("stat", [P, 6, NT])
        first_i = sb("first_i", [1, NG], I32)
        first_f = sb("first_f", [1, NG])
        base_f = sb("base_f", [1, NG])
        base_i = sb("base_i", [1, NG], I32)
        base = sb("base", [P, NG])
        rel_hi = sb("rel_hi", [P, NG])
        rel_lo = sb("rel_lo", [P, NG])
        back = sb("back", [1, NG])
        bad = sb("bad", [P, 3])
        last_neg = sb("last_neg", [P, 1])
        wsum = sb("wsum", [P, 2])
        zp = sb("zp", [P, 1])
        w2T = sb("w2T", [U, U + 1])
        ww = sb("ww", [U + 1, U])
        wws = sb("wws", [U + 1, U])
        bad1 = sb("bad1", [1, 4])
        flag = sb("flag", [1, 1], I32)
        src_i = sb("src_i", [P, 2, TG], I32)
        dst_i = sb("dst_i", [P, 2, TG], I32)
        ef_sb = sb("ef_sb", [P, 2, TG * DE])
        q_win = sb("q_win", [P, 2, H2])
        p_rows = sb("p_rows", [P, 2, TG * H2])
        rel = sb("rel", [P, 2, TG])
        relT = sb("relT", [TG, P], BF16)
        hot = sb("hot", [P, 2, TG * WIN])
        comb = sb("comb", [P, 2, TG * P])
        z = sb("z", [P, TG, H2])
        th = sb("th", [P, TG, H2])
        s2 = sb("s2", [P, TG, H2])
        lg = sb("lg", [P, TG])
        lgb = sb("lgb", [P, TG])
        pmax = sb("pmax", [P, 1])
        gmax = sb("gmax", [1, 1])
        neg_max = sb("neg_max", [P, NG])
        fade = sb("fade", [P, 2])
        w = sb("w", [P, TG])
        wm = sb("wm", [P, TG])
        v = sb("v", [P, TG, U + 1])
        acc = sb("acc", [U + 1, NP])
        ref = sb("ref", [U + 1, NP])
        rows65 = U + 1
        zall = sb("zall", [P, 1])
        rz = sb("rz", [P, 1])
        su = sb("su", [U + 1, 2, NBT * P])
        h_p, h_q = (flat(z)[0:D + 1, k * NBT * P:(k + 2) * NBT * P].rearrange("p (a n) -> p a n", a=2) for k in (0, 2))
        pr, qr = (flat(th)[:, k * NBT * H2:(k + 2) * NBT * H2].rearrange("p (a t u) -> p a t u", a=2, t=NBT) for k in (0, 2))
        xc = flat(p_rows)[:, 0:NT * D].rearrange("p (t d) -> p t d", d=D)
        sq = flat(comb)[:, 0:NT * D].rearrange("p (t d) -> p t d", d=D)
        hn = flat(comb)[:, NT * D:(NT + 2 * NBT) * D].rearrange("p (a t d) -> p a t d", a=2, t=NBT)
        thu = flat(th)[0:U, 0:2 * NBT * P].rearrange("p (a n) -> p a n", a=2)
        y = flat(s2)[:, 0:2 * NBT * D].rearrange("p (a t d) -> p a t d", a=2, t=NBT)
        hot_g = flat(hot)[:, 0:TG * P].rearrange("p (t n) -> p t n", t=TG)

        bank = [ctx.enter_context(nc.psum_tensor(f"bank{i}", [P, 512], F32)) for i in range(6)]
        ps_prep = ctx.enter_context(nc.psum_tensor("ps_prep", [P, 1024], F32))
        ps_efT = ps_prep[:, 0:TG * DE]
        ps_relT = ps_prep[0:TG, TG * DE:TG * DE + P]
        ps_row = bank[0:2]
        ps_z = bank[2:4]
        ps_part = bank[4]
        ps_small = bank[5]
        ps_hT = bank[0:2]
        ps_p = bank[2:4]
        ps_q = [bank[4], ps_prep[:, 0:512]]
        ps_uh = bank[0:2]
        ps_ww = bank[5]
        ps_u = bank[2:4]
        ps_y = [bank[4], ps_prep[:, 0:512]]

        (zeroed, ident_ok, const_ok, sel_ok, w_ld, w_ld2, first_ld, halved, low_ok, dve_step) = (
            sem(n) for n in ("zeroed", "ident_ok", "const_ok", "sel_ok", "w_ld", "w_ld2", "first_ld", "halved", "low_ok", "dve_step"))
        xc_ok, sq_ok, std_ok, ww_done, ww_ok, scale_ok = (
            sem(n) for n in ("xc_ok", "sq_ok", "std_ok", "ww_done", "ww_ok", "scale_ok"))
        x_ld = [sem("x_ld0"), sem("x_ld1")]
        (base_ok, baseB_done, baseB_ok, var_ok, rstd_ok, hn_ok, hT_done, hst_ok, hT_ok, p_done, p_ok, hq_ok, q_done, q_ok, uh_done, uh_ok) = (
            sem(n) for n in ("base_ok", "baseB_done", "baseB_ok", "var_ok", "rstd_ok", "hn_ok", "hT_done", "hst_ok", "hT_ok",
                             "p_done", "p_ok", "hq_ok", "q_done", "q_ok", "uh_done", "uh_ok"))
        p_st = [sem("p_st0"), sem("p_st1")]
        q_st = [sem("q_st0"), sem("q_st1")]
        ld = [sem("ld0"), sem("ld1")]
        src_ld = [sem("src_ld0"), sem("src_ld1")]
        win_ld = [sem("win_ld0"), sem("win_ld1")]
        gath = [[sem(f"gath{a}{q}") for q in range(NQ)] for a in range(2)]
        (rel_ok, hot_ok, prep_done, efT_ok, relT_ok, row_done, abs_ok, comb_ok) = (
            sem(n) for n in ("rel_ok", "hot_ok", "prep_done", "efT_ok", "relT_ok", "row_done", "abs_ok", "comb_ok"))
        (z_done, z_ok, th_ok, s_ok, prod_ok, lgq_ok, lg_ok, pmax_ok, maxT_done, gmax_ok, maxB_done, negm_ok) = (
            sem(n) for n in ("z_done", "z_ok", "th_ok", "s_ok", "prod_ok", "lgq_ok", "lg_ok", "pmax_ok", "maxT_done",
                             "gmax_ok", "maxB_done", "negm_ok"))
        (w_ok, wm_ok, v_ok, part_done, acc_ok, ref_ok) = (
            sem(n) for n in ("w_ok", "wm_ok", "v_ok", "part_done", "acc_ok", "ref_ok"))
        (bad_ok, badT_done, flag_ok) = (sem(n) for n in ("bad_ok", "badT_done", "flag_ok"))
        (sums_ok, refx_ok, scaled_ok, zall_done, zall_ok, rz_ok) = (
            sem(n) for n in ("sums_ok", "refx_ok", "scaled_ok", "zall_done", "zall_ok", "rz_ok"))
        (u_done, u_ok, thu_ok, su_ok, y_done, y_ok) = (
            sem(n) for n in ("u_done", "u_ok", "thu_ok", "su_ok", "y_done", "y_ok"))
        out_st = [sem("out_st0"), sem("out_st1")]
        (g_start, g_ld, g_gath, g_prep, g_efT, g_z, g_zok, g_th, g_pmax, g_maxT, g_gmax, g_maxB, g_negm, g_w, g_v, g_hot, g_part,
         g_acc, g_step) = (
            sem("g_" + n) for n in ("start", "ld", "gath", "prep", "efT", "z", "zok", "th", "pmax", "maxT", "gmax", "maxB", "negm",
                                    "w", "v", "hot", "part", "acc", "step"))
        turn = sem("turn")
        ext_ok, g_acc0, g_dve, g_silu, g_rel = sem("ext_ok"), sem("g_acc0"), sem("g_dve"), sem("g_silu"), sem("g_rel")

        def wait(eng, s, n):
            if not (isinstance(n, int) and n <= 0):
                eng.wait_ge(s, n)

        def groups(eng, body):
            body(0, 0)
            body(1, 1)
            with eng.Fori(1, LAST // 2 - 1) as pair:
                body(pair * 2, 0)
                body(pair * 2 + 1, 1)
            body(LAST - 2, 0)
            body(LAST - 1, 1)
            body(LAST, 0)

        def batches(eng, body):
            body(0, 0, NBT)
            body(1, 1, NBT)
            with eng.Fori(1, NB // 2 - 1) as pair:
                body(pair * 2, 0, NBT)
                body(pair * 2 + 1, 1, NBT)
            body(NB - 2, 0, NBT)
            body(NB - 1, 1, NBT)
            body(NB, 0, 1)

        def is_last(g):
            return isinstance(g, int) and g == LAST

        def following(g):
            return tuple(g + k if not isinstance(g, int) or g + k <= LAST else None for k in (1, 2))

        def tiles(g):
            return TL if is_last(g) else TG

        def edge0(g):
            return E - TL * P if is_last(g) else g * GE

        def per(a, g, n):
            return (g - a) * (n // 2) + n

        def stored(eng, st):
            eng.wait_ge(st[0], 16 * (NB // 2 + 1))
            eng.wait_ge(st[1], 16 * (NB // 2))

        def nodes_of(b, ahead):
            if not isinstance(b, int) or b + ahead < NB:
                return NBT
            return 1 if b + ahead == NB else 0

        def parts(t, q):
            return t[:, q * TQ:(q + 1) * TQ, :]

        def load_src(eng, g, a, s):
            e0, T = edge0(g), tiles(g)
            eng.dma_start(src_i[:, a, 0:T], src[bass.ds(e0, T * P)].rearrange("(p t) -> p t", t=T)).then_inc(s, 16)

        def load_edges(eng, g, a, s):
            e0, T = edge0(g), tiles(g)
            eng.dma_start(dst_i[:, a, 0:T], dst[bass.ds(e0, T * P)].rearrange("(p t) -> p t", t=T)).then_inc(s, 16)
            eng.dma_start(ef_sb[:, a, 0:T * DE], ef[bass.ds(e0, T * P), :].rearrange("(p t) f -> p (t f)", t=T)).then_inc(s, 16)

        x_t = x[0:(NT - 1) * P, :].rearrange("(t p) d -> p t d", p=P)
        p_t = p_tab[0:(NT - 1) * P, :].rearrange("(t p) d -> p t d", p=P)
        q_t = q_tab[0:(NT - 1) * P, :].rearrange("(t p) d -> p t d", p=P)
        out_t = out[0:(NT - 1) * P, :].rearrange("(t p) d -> p t d", p=P)
        WS = 16 * (2 * 2 + 9)

        block = ctx.enter_context(nc.Block())

        @block.sync
        def _(sp):
            h0, h1 = HALVES[0][1], HALVES[1][1]
            sp.dma_start(x_sb[:, 0:h0, :], x_t[:, 0:h0, :]).then_inc(x_ld[0], 16)
            sp.dma_start(x_sb[:, h0:h1 - 1, :], x_t[:, h0:h1 - 1, :]).then_inc(x_ld[1], 16)
            sp.wait_ge(zeroed, 1)
            sp.dma_start(x_sb[0:LT, NT - 1, :], x[(NT - 1) * P:N, :]).then_inc(x_ld[1], 16)
            with nc.allow_non_contiguous_dma(reason="one dst of each group"):
                sp.dma_start(first_i[:, 0:LAST], dst[0:LAST * GE].rearrange("(a g e) -> a g e", a=1, e=GE)[:, :, 0]).then_inc(first_ld, 16)
            sp.dma_start(first_i[:, LAST:NG], dst[E - TL * P:E - TL * P + 1][None, :]).then_inc(first_ld, 16)
            for a in range(2):
                sp.dma_start(q_win[WIN:P, a, 0:U], W1[2 * D:2 * D + DE, :]).then_inc(w_ld2, 16)
                sp.dma_start(q_win[WIN:P, a, U:H2], Wa1[2 * D:2 * D + DE, :]).then_inc(w_ld2, 16)

            def load_group(g, a):
                wait(sp, prep_done, g - 1)
                load_edges(sp, g, a, ld[a])
                if not (isinstance(g, int) and g < 2):
                    sp.wait_ge(gath[a][NQ - 1], per(a, g - 2, 16 * TQ))
                load_src(sp, g, a, src_ld[a])
            load_group(0, 0)
            load_group(1, 1)

            def store_rows(tab, tab_t, rows, rows_ok, st):
                def store(b, a, nt):
                    sp.wait_ge(rows_ok, b + 1)
                    if nt > 1:
                        sp.dma_start(tab_t[:, bass.ds(b * NBT, NBT), :], rows[:, a, :, :]).then_inc(st[a], 16)
                    else:
                        sp.dma_start(tab[(NT - 1) * P:N, :], rows[0:LT, a, 0, :]).then_inc(st[a], 16)
                return store
            batches(sp, store_rows(p_tab, p_t, pr, p_ok, p_st))
            batches(sp, store_rows(q_tab, q_t, qr, q_ok, q_st))
            groups(sp, lambda g, a: None if isinstance(g, int) and g < 2 else load_group(g, a))

            def store_out(b, a, nt):
                sp.wait_ge(y_ok, b + 1)
                if nt > 1:
                    sp.dma_start(out_t[:, bass.ds(b * NBT, NBT), :], y[:, a, :, :]).then_inc(out_st[a], 16)
                else:
                    sp.dma_start(out[(NT - 1) * P:N, :], y[0:LT, a, 0, :]).then_inc(out_st[a], 16)
            batches(sp, store_out)
            sp.wait_ge(out_st[0], 16 * (NB // 2 + 1))
            sp.wait_ge(out_st[1], 16 * (NB // 2))

        @block.gpsimd
        def _(pool):
            nc.gpsimd.memset(x_sb[:, NT - 1, :], 0.0).then_inc(zeroed, 1)
            nc.gpsimd.memset(ones[:], 1.0).then_inc(const_ok, 1)
            nc.gpsimd.memset(ident[:], 0.0).then_inc(zeroed, 1)
            nc.gpsimd.memset(mask[:], 0.0).then_inc(zeroed, 1)
            nc.gpsimd.iota(iota[:], [[1, P]], base=0, channel_multiplier=0, allow_small_or_imprecise_dtypes=True).then_inc(const_ok, 1)
            nc.gpsimd.iota(row_no[:], [[0, 1]], base=0, channel_multiplier=-1, allow_small_or_imprecise_dtypes=True).then_inc(const_ok, 1)
            pool.wait_ge(zeroed, 3)
            nc.gpsimd.affine_select(out=ident[:], in_=ident[:], compare_op=ALU.not_equal, fill=1.0,
                                    base=0, pattern=[[-1, P]], channel_multiplier=1).then_inc(ident_ok, 1)
            nc.gpsimd.affine_select(out=mask[:], in_=mask[:], compare_op=ALU.is_gt, fill=1.0,
                                    base=DUP, pattern=[[-1, TL]], channel_multiplier=-TL).then_inc(const_ok, 1)
            pool.wait_ge(ident_ok, 1)
            pool.wait_ge(const_ok, 4)
            nc.gpsimd.memset(h_q[D:D + 1, :, :], 1.0).then_inc(const_ok, 1)
            pool.wait_ge(const_ok, 5)
            nc.gpsimd.memset(hT[D:D + 1, :], 1.0).then_inc(const_ok, 1)
            pool.wait_ge(const_ok, 6)
            nc.gpsimd.memset(su[U:U + 1, :, :], 1.0).then_inc(const_ok, 1)
            pool.wait_ge(const_ok, 7)
            nc.gpsimd.memset(acc[:], 0.0).then_inc(low_ok, 1)
            nc.gpsimd.memset(ref[:], LOW).then_inc(low_ok, 1)
            stored(pool, p_st)

            def gather(g, a):
                pool.wait_ge(src_ld[a], per(a, g, 16))
                for q in range(tiles(g) // TQ):
                    if not (isinstance(g, int) and g < 2):
                        pool.wait_ge(z_ok, (g - 2) * NQ + q + 1)
                        pool.sem_inc(turn, 1)
                    for t in range(q * TQ, (q + 1) * TQ):
                        pool.indirect_dma_start(p_rows[:, a, t * H2:(t + 1) * H2], None, p_tab,
                                                bass.IndirectOffsetOnAxis(src_i[:, a, t:t + 1], 0)).then_inc(gath[a][q], 16)
            groups(pool, gather)

            stored(pool, q_st)
            pool.wait_ge(flag_ok, 1)
            misfit = pool.value_load(flag[0:1, 0:1], min_val=0, max_val=1)
            with pool.If(misfit == 1):
                nc.gpsimd.iota(tile0[:], [[P, NT]], base=0, channel_multiplier=0,
                               allow_small_or_imprecise_dtypes=True).then_inc(g_step, 1)

                def gather_all(g):
                    pool.wait_ge(g_start, g + 1)
                    load_src(pool, g, 0, g_ld)
                    load_edges(pool, g, 0, g_ld)
                    pool.wait_ge(g_ld, (g + 1) * 48)
                    pool.sem_inc(turn, 1)
                    for t in range(tiles(g)):
                        pool.indirect_dma_start(p_rows[:, 0, t * H2:(t + 1) * H2], None, p_tab,
                                                bass.IndirectOffsetOnAxis(src_i[:, 0, t:t + 1], 0)).then_inc(g_gath, 16)
                        pool.indirect_dma_start(p_rows[:, 1, t * H2:(t + 1) * H2], None, q_tab,
                                                bass.IndirectOffsetOnAxis(dst_i[:, 0, t:t + 1], 0)).then_inc(g_gath, 16)
                gather_all(0)
                with pool.Fori(1, LAST) as g:
                    gather_all(g)
                gather_all(LAST)

        @block.scalar
        def _(act):
            act.dma_start(w_p[:, 0:U], W1[0:D, :]).then_inc(w_ld, 16)
            act.dma_start(w_p[:, U:H2], Wa1[0:D, :]).then_inc(w_ld, 16)
            act.dma_start(w_q[0:D, 0:U], W1[D:2 * D, :]).then_inc(w_ld, 16)
            act.dma_start(w_q[0:D, U:H2], Wa1[D:2 * D, :]).then_inc(w_ld, 16)
            act.dma_start(w_q[D:D + 1, 0:U], b1[None, :]).then_inc(w_ld, 16)
            act.dma_start(w_q[D:D + 1, U:H2], ba1[None, :]).then_inc(w_ld, 16)
            act.dma_start(wa2[:], Wa2.rearrange("a b -> b a").broadcast_to([P, U])).then_inc(w_ld2, 16)
            act.dma_start(ba2c[:], ba2[None, :].broadcast_to([P, 1])).then_inc(w_ld2, 16)
            act.dma_start(w2e[0:U, :], W2).then_inc(w_ld2, 16)
            act.dma_start(w2e[U:U + 1, :], b2[None, :]).then_inc(w_ld2, 16)
            act.dma_start(wu1h[0:D, :], Wu1[0:D, :]).then_inc(w_ld2, 16)
            act.dma_start(wu1h[D:D + 1, :], bu1[None, :]).then_inc(w_ld2, 16)
            act.dma_start(wu1a[:], Wu1[D:D + U, :]).then_inc(w_ld2, 16)
            act.dma_start(wu2e[0:U, :], Wu2).then_inc(w_ld2, 16)
            act.dma_start(wu2e[U:U + 1, :], bu2[None, :]).then_inc(w_ld2, 16)

            for h, (t0, t1) in enumerate(HALVES):
                act.wait_ge(xc_ok, h + 1)
                nc.scalar.activation(sq[:, t0:t1, :], xc[:, t0:t1, :], ACT.Square).then_inc(sq_ok, 1)
            act.wait_ge(var_ok, len(HALVES))
            nc.scalar.activation(stat[:, 3, :], stat[:, 0, :], ACT.Sqrt).then_inc(std_ok, 1)

            def node_rows(b, a, nt):
                n = nt * P
                act.wait_ge(hT_done, b + 1)
                wait(act, p_done, b - 1)
                nc.scalar.activation(h_p[0:D, a, 0:n], ps_hT[a][0:D, 0:n], ACT.Relu).then_inc(hst_ok, 1)
                nc.scalar.activation(hT[0:D, bass.ds(b * NBT * P, n)], ps_hT[a][0:D, 0:n], ACT.Relu).then_inc(hT_ok, 1)
            batches(act, node_rows)

            def copy_h(b, a, nt):
                wait(act, q_done, b - 1)
                act.sem_inc(turn, 1)
                nc.scalar.activation(h_q[0:D, a, 0:nt * P], hT[0:D, bass.ds(b * NBT * P, nt * P)], ACT.Copy).then_inc(hq_ok, 1)

            def node_units(b, a, nt):
                if nodes_of(b, 1):
                    copy_h(b + 1, 1 - a, nodes_of(b, 1))
                act.wait_ge(uh_done, b + 1)
                act.sem_inc(turn, 1)
                nc.scalar.activation(hT[0:D, bass.ds(b * NBT * P, nt * P)], ps_uh[a][0:U, 0:nt * P], ACT.Copy).then_inc(uh_ok, 1)
            act.wait_ge(hT_ok, NB + 1)
            copy_h(0, 0, NBT)
            batches(act, node_units)

            def window(g, a):
                wait(act, z_done, (g - 1) * NQ)
                node = act.value_load(base_i[0:1, bass.ds(g, 1)], min_val=0, max_val=N - WIN)
                act.dma_start(q_win[0:WIN, a, :], q_tab[bass.ds(node, WIN), :]).then_inc(win_ld[a], 16)

            def copy_efT(dst_a, T):
                for j in range(TQ):
                    last = nc.scalar.copy(comb[WIN:P, dst_a, 0:T * P].rearrange("p (q j e) -> p q j e", j=TQ, e=P)[:, :, j, :],
                                          ps_prep[j * DE:(j + 1) * DE, 0:T * DE].rearrange("p (q e) -> p q e", e=P))
                return last

            def copy_relT(g, a):
                act.wait_ge(prep_done, g + 1)
                wait(act, row_done, g * NQ)
                nc.scalar.copy(relT[0:tiles(g), :], ps_relT[0:tiles(g), :]).then_inc(relT_ok, 1)

            def one_hots(g, a, qs):
                qs = [q for q in qs if q < tiles(g) // TQ]
                for q in qs:
                    bank_q = ps_row[(q + a) % 2][0:WIN, :]
                    act.wait_ge(row_done, g * NQ + q + 1)
                    nc.scalar.activation(bank_q, bank_q, ACT.Abs, bias=row_no[0:WIN, :]).then_inc(abs_ok, 1)
                for q in qs:
                    act.wait_ge(abs_ok, g * NQ + q + 1)
                    nc.scalar.activation(comb[0:WIN, a, q * 512:(q + 1) * 512], ps_row[(q + a) % 2][0:WIN, :], ACT.Relu,
                                         scale=-1.0, bias=ones[0:WIN, 0:1]).then_inc(comb_ok, 1)

            stored(act, q_st)
            act.wait_ge(base_ok, 1)
            act.wait_ge(const_ok, 7)
            window(0, 0)
            copy_relT(0, 0)
            copy_efT(0, TG).then_inc(efT_ok, 1)
            for qs in ([0, 1], [2, 3], [4]):
                one_hots(0, 0, qs)
            copy_relT(1, 1)

            def group(g, a):
                nxt, nxt2 = following(g)
                if nxt is not None:
                    window(nxt, 1 - a)
                for q in range(tiles(g) // TQ):
                    act.wait_ge(z_ok, g * NQ + q + 1)
                    nc.scalar.activation(parts(th, q), parts(z, q), ACT.Tanh, scale=0.5).then_inc(th_ok, 1)
                    if nxt is not None:
                        if q == 0:
                            copy_efT(1 - a, tiles(nxt)).then_inc(efT_ok, 1)
                        else:
                            one_hots(nxt, 1 - a, ([0, 1], [2, 3], [4], [])[q - 1])
                act.wait_ge(negm_ok, g + 1)
                nm = neg_max[:, bass.ds(g, 1)]
                nc.scalar.activation(w[:, 0:tiles(g)], lgb[:, 0:tiles(g)], ACT.Exp, bias=nm).then_inc(w_ok, 1)
                if not (isinstance(g, int) and g == 0):
                    nc.scalar.activation(fade[:, a:a + 1], neg_max[:, bass.ds(g - 1, 1)], ACT.Exp, scale=-1.0, bias=nm).then_inc(w_ok, 1)
                else:
                    nc.scalar.activation(fade[:, a:a + 1], row_no[:], ACT.Exp).then_inc(w_ok, 1)
                if nxt2 is not None:
                    copy_relT(nxt2, a)
            groups(act, group)

            act.wait_ge(flag_ok, 1)
            misfit = act.value_load(flag[0:1, 0:1], min_val=0, max_val=1)
            with act.If(misfit == 1):
                def group_any(g):
                    act.wait_ge(g_prep, g + 1)
                    copy_efT(0, tiles(g)).then_inc(g_efT, 1)
                    for q in range(tiles(g) // TQ):
                        act.wait_ge(g_zok, g * NQ + q + 1)
                        nc.scalar.activation(parts(th, q), parts(z, q), ACT.Tanh, scale=0.5).then_inc(g_th, 1)
                    act.wait_ge(g_negm, g + 1)
                    nc.scalar.activation(w[:, 0:tiles(g)], lgb[:, 0:tiles(g)], ACT.Exp, bias=neg_max[:, 1:2]).then_inc(g_w, 1)
                    nc.scalar.activation(fade[:, 0:1], neg_max[:, 0:1], ACT.Exp, scale=-1.0, bias=neg_max[:, 1:2]).then_inc(g_w, 1)
                group_any(0)
                with act.Fori(1, LAST) as g:
                    group_any(g)
                group_any(LAST)

            act.wait_ge(sums_ok, 1)

            def fade_ref(b, a, nt):
                c = bass.ds(b * NBT * P, nt * P)
                nc.scalar.activation(ref[:, c], ref[:, c], ACT.Exp, bias=last_neg[0:rows65, :]).then_inc(refx_ok, 1)

            def update(b, a, nt):
                n = nt * P
                act.wait_ge(u_ok, b + 1)
                wait(act, su_ok, b - 1)
                act.sem_inc(turn, 1)
                nc.scalar.activation(thu[:, a, 0:n], hT[0:U, bass.ds(b * NBT * P, n)], ACT.Tanh, scale=0.5).then_inc(thu_ok, 1)
                if nodes_of(b, 2):
                    fade_ref(b + 2, a, nodes_of(b, 2))
            for b in range(2):
                fade_ref(b, b % 2, NBT)
            batches(act, update)

        @block.tensor
        def _(pe):
            pe.wait_ge(ident_ok, 1)
            pe.wait_ge(w_ld, 96)

            def transpose_rows(b, a, nt):
                pe.wait_ge(hn_ok, b + 1)
                wait(pe, hT_ok, b - 1)
                pe.sem_inc(turn, 1)
                for t in range(NBT):
                    last = nc.tensor.transpose(ps_hT[a][0:D, t * P:(t + 1) * P], hn[:, a, t, :], ident[:])
                last.then_inc(hT_done, 1)

            def node_rows(b, a, nt):
                if nodes_of(b, 1):
                    transpose_rows(b + 1, 1 - a, nodes_of(b, 1))
                pe.wait_ge(hst_ok, b + 1)
                wait(pe, p_ok, b - 1)
                for t in range(nt):
                    last = nc.tensor.matmul(ps_p[a][:, t * H2:(t + 1) * H2], h_p[0:D, a, t * P:(t + 1) * P], w_p[:], start=True, stop=True)
                last.then_inc(p_done, 1)
            transpose_rows(0, 0, NBT)
            batches(pe, node_rows)
            pe.wait_ge(const_ok, 7)
            pe.wait_ge(base_ok, 1)
            nc.tensor.matmul(ps_small[:, 0:NG], ones[0:1, :], base_f[:], start=True, stop=True).then_inc(baseB_done, 1)
            pe.wait_ge(w_ld2, WS)

            def node_units(b, a, nt):
                pe.wait_ge(hq_ok, b + 1)
                wait(pe, q_ok, b - 1)
                for t in range(nt):
                    last = nc.tensor.matmul(ps_q[a][:, t * H2:(t + 1) * H2], h_q[:, a, t * P:(t + 1) * P], w_q[:], start=True, stop=True)
                last.then_inc(q_done, 1)
                wait(pe, uh_ok, b - 1)
                nc.tensor.matmul(ps_uh[a][0:U, 0:nt * P], wu1h[:], hT[:, bass.ds(b * NBT * P, nt * P)], start=True, stop=True).then_inc(uh_done, 1)
            batches(pe, node_units)
            pe.wait_ge(baseB_ok, 1)
            pe.wait_ge(sel_ok, 1)
            pe.wait_ge(uh_ok, NB + 1)
            pe.wait_ge(q_ok, NB + 1)
            pe.wait_ge(p_ok, NB + 1)
            pe.wait_ge(halved, 3)
            nc.tensor.transpose(ps_ww[0:U, 0:rows65], w2e[:], ident[0:rows65, 0:rows65]).then_inc(ww_done, 1)
            pe.wait_ge(ww_ok, 1)
            nc.tensor.matmul(ps_ww[0:rows65, 0:U], w2T[:], wu1a[:], start=True, stop=True).then_inc(ww_done, 1)
            pe.wait_ge(ww_ok, 2)

            def transpose_ef(a, T):
                for q in range(T // TQ):
                    last = nc.tensor.transpose(ps_prep[:, q * P:(q + 1) * P], ef_sb[:, a, q * P:(q + 1) * P], ident[:])
                return last

            def prepare(g, a):
                pe.wait_ge(rel_ok, g + 1)
                pe.wait_ge(ld[a], per(a, g, 32))
                wait(pe, efT_ok, g)
                pe.sem_inc(turn, 1)
                transpose_ef(a, tiles(g))
                nc.tensor.transpose(ps_relT[0:tiles(g), :], rel[:, a, 0:tiles(g)], ident[:]).then_inc(prep_done, 1)

            def spread(g, a, qs):
                T = tiles(g)
                for q in [q for q in qs if q < T // TQ]:
                    if q == 0:
                        pe.wait_ge(relT_ok, g + 1)
                    wait(pe, comb_ok, g * NQ + q - 1)
                    pe.sem_inc(turn, 1)
                    for t in range(q * TQ, (q + 1) * TQ):
                        last = nc.tensor.matmul(ps_row[(q + a) % 2][:, (t % TQ) * P:(t % TQ + 1) * P], sel[0:T, t, :], relT[0:T, :], start=True, stop=True)
                    last.then_inc(row_done, 1)

            prepare(0, 0)
            for qs in ([0, 1], [2, 3], [4]):
                spread(0, 0, qs)
            prepare(1, 1)

            def zmm(g, a, q):
                if q == 0:
                    pe.wait_ge(efT_ok, g + 1)
                    pe.wait_ge(win_ld[a], per(a, g, 16))
                wait(pe, z_ok, g * NQ + q - 1)
                pe.wait_ge(comb_ok, g * NQ + q + 1)
                for t in range(q * TQ, (q + 1) * TQ):
                    last = nc.tensor.matmul(ps_z[(q + a) % 2][:, (t % TQ) * H2:(t % TQ + 1) * H2], comb[:, a, t * P:(t + 1) * P], q_win[:, a, :],
                                            start=True, stop=True)
                last.then_inc(z_done, 1)

            def sums(g, a, t0, t1):
                T = tiles(g)
                for t in range(t0, min(t1, T)):
                    last = nc.tensor.matmul(ps_part[0:rows65, 0:WIN], v[:, t, :], hot[:, a, t * WIN:(t + 1) * WIN], start=(t == 0), stop=(t == T - 1))
                    if t == T - 1:
                        last.then_inc(part_done, 1)

            def group(g, a):
                nxt, nxt2 = following(g)
                if nxt is not None:
                    spread(nxt, 1 - a, [0, 1])
                    zmm(g, a, 4)
                    spread(nxt, 1 - a, [2, 3, 4])
                else:
                    pe.wait_ge(bad_ok, 1)
                    nc.tensor.transpose(ps_small[0:1, P:2 * P], bad[:, 2:3], ident[:]).then_inc(badT_done, 1)
                pe.wait_ge(pmax_ok, g + 1)
                nc.tensor.transpose(ps_small[0:1, 0:P], pmax[:], ident[:]).then_inc(maxT_done, 1)
                if nxt is not None:
                    zmm(nxt, 1 - a, 0)
                    zmm(nxt, 1 - a, 1)
                pe.wait_ge(gmax_ok, g + 1)
                nc.tensor.matmul(ps_small[:, 0:1], ones[0:1, :], gmax[:], start=True, stop=True).then_inc(maxB_done, 1)
                if nxt2 is not None:
                    prepare(nxt2, a)
                if nxt is not None:
                    zmm(nxt, 1 - a, 2)
                pe.wait_ge(v_ok, g + 1)
                pe.wait_ge(hot_ok, g + 1)
                wait(pe, acc_ok, g)
                sums(g, a, 0, TG // 2)
                if nxt is not None and tiles(nxt) > 3 * TQ:
                    zmm(nxt, 1 - a, 3)
                sums(g, a, TG // 2, TG)
            for q in range(4):
                zmm(0, 0, q)
            groups(pe, group)

            pe.wait_ge(flag_ok, 1)
            misfit = pe.value_load(flag[0:1, 0:1], min_val=0, max_val=1)
            with pe.If(misfit == 1):
                def group_any(g):
                    pe.wait_ge(g_ld, (g + 1) * 48)
                    pe.sem_inc(turn, 1)
                    T = tiles(g)
                    transpose_ef(0, T).then_inc(g_prep, 1)
                    pe.wait_ge(g_efT, g + 1)
                    for q in range(T // TQ):
                        wait(pe, g_zok, g * NQ + q - 1)
                        pe.sem_inc(turn, 1)
                        for t in range(q * TQ, (q + 1) * TQ):
                            last = nc.tensor.matmul(ps_z[q % 2][:, (t % TQ) * H2:(t % TQ + 1) * H2], comb[WIN:P, 0, t * P:(t + 1) * P], q_win[WIN:P, 0, :],
                                                    start=True, stop=True)
                        last.then_inc(g_z, 1)
                    pe.wait_ge(g_pmax, g + 1)
                    nc.tensor.transpose(ps_small[0:1, 0:P], pmax[:], ident[:]).then_inc(g_maxT, 1)
                    pe.wait_ge(g_gmax, g + 1)
                    nc.tensor.matmul(ps_small[:, 0:1], ones[0:1, :], gmax[:], start=True, stop=True).then_inc(g_maxB, 1)
                    pe.wait_ge(g_v, g + 1)

                    def tile_sums(i):
                        pe.wait_ge(g_hot, i + 1)
                        for t in range(T):
                            last = nc.tensor.matmul(ps_part[0:rows65, 0:P], v[:, t, :], hot_g[:, t, :], start=(t == 0), stop=(t == T - 1))
                        last.then_inc(g_part, 1)
                    pe.sem_inc(turn, 1)
                    with pe.Fori(0, NT) as i:
                        tile_sums(g * NT + i)
                group_any(0)
                with pe.Fori(1, LAST) as g:
                    group_any(g)
                group_any(LAST)

            pe.wait_ge(sums_ok, 1)
            nc.tensor.matmul(ps_small[:, 0:1], ones[:], zp[:], start=True, stop=True).then_inc(zall_done, 1)
            pe.wait_ge(scale_ok, 1)

            def aggregate(b, a, nt):
                pe.wait_ge(scaled_ok, b + 1)
                wait(pe, u_ok, b - 1)
                nc.tensor.matmul(ps_u[a][0:U, 0:nt * P], wws[:], acc[:, bass.ds(b * NBT * P, nt * P)], start=True, stop=True).then_inc(u_done, 1)

            def update(b, a, nt):
                if nodes_of(b, 2):
                    aggregate(b + 2, a, nodes_of(b, 2))
                pe.wait_ge(su_ok, b + 1)
                wait(pe, y_ok, b - 1)
                for t in range(nt):
                    last = nc.tensor.matmul(ps_y[a][:, t * D:(t + 1) * D], su[:, a, t * P:(t + 1) * P], wu2e[:], start=True, stop=True)
                last.then_inc(y_done, 1)
            aggregate(0, 0, NBT)
            aggregate(1, 1, NBT)
            batches(pe, update)

        @block.vector
        def _(dve):
            steps = [0]

            def chain(ins):
                steps[0] += 1
                ins.then_inc(dve_step, 1)
                dve.wait_ge(dve_step, steps[0])

            for h, (t0, t1) in enumerate(HALVES):
                ts, big = slice(t0, t1), [P, t1 - t0, D]
                dve.wait_ge(x_ld[h], 16 * (h + 1))
                chain(nc.vector.tensor_reduce(stat[:, 0, ts], x_sb[:, ts, :], AX.X, ALU.add))
                chain(nc.vector.tensor_scalar(stat[:, 1, ts], stat[:, 0, ts], 1.0 / D, None, ALU.mult))
                nc.vector.tensor_tensor(xc[:, ts, :], x_sb[:, ts, :], stat[:, 1, ts].unsqueeze(2).broadcast_to(big), ALU.subtract).then_inc(xc_ok, 1)
            for h, (t0, t1) in enumerate(HALVES):
                ts = slice(t0, t1)
                dve.wait_ge(sq_ok, h + 1)
                chain(nc.vector.tensor_reduce(stat[:, 2, ts], sq[:, ts, :], AX.X, ALU.add))
                nc.vector.tensor_scalar(stat[:, 0, ts], stat[:, 2, ts], 1.0 / D, EPS, ALU.mult, ALU.add).then_inc(var_ok, 1)
            dve.wait_ge(std_ok, 1)
            var, std, inv, t1, t2 = (stat[:, i, :] for i in (0, 3, 4, 1, 2))
            chain(nc.vector.reciprocal(inv, std))
            chain(nc.vector.tensor_tensor(t1, var, inv, ALU.mult))
            chain(nc.vector.tensor_tensor(t2, t1, inv, ALU.mult))
            chain(nc.vector.tensor_scalar(t1, t2, -0.5, 1.5, ALU.mult, ALU.add))
            nc.vector.tensor_tensor(stat[:, 5, :], inv, t1, ALU.mult).then_inc(rstd_ok, 1)

            def normalise(b, a, nt):
                wait(dve, hT_done, b - 1)
                ts = bass.ds(b * NBT, nt)
                nc.vector.tensor_tensor(hn[:, a, 0:nt, :], xc[:, ts, :], stat[:, 5, ts].unsqueeze(2).broadcast_to([P, nt, D]), ALU.mult).then_inc(hn_ok, 1)

            def node_rows(b, a, nt):
                if nodes_of(b, 2):
                    normalise(b + 2, a, nodes_of(b, 2))
                dve.wait_ge(p_done, b + 1)
                wait(dve, p_st[a], 8 * (b - a))
                nc.vector.tensor_copy(pr[:, a, 0:nt, :], ps_p[a][:, 0:nt * H2]).then_inc(p_ok, 1)
            dve.wait_ge(rstd_ok, 1)
            normalise(0, 0, NBT)
            normalise(1, 1, NBT)
            batches(dve, node_rows)
            dve.wait_ge(first_ld, 32)
            chain(nc.vector.tensor_copy(first_f[:], first_i[:]))
            chain(nc.vector.tensor_scalar(base_f[:], first_f[:], float(N - WIN), None, ALU.min))
            nc.vector.tensor_copy(base_i[:], base_f[:]).then_inc(base_ok, 1)
            chain(nc.vector.tensor_tensor(back[:, 0:LAST], base_f[:, 0:LAST], base_f[:, 1:NG], ALU.subtract))
            chain(nc.vector.tensor_reduce(bad1[:, 0:1], back[:, 0:LAST], AX.X, ALU.max))
            dve.wait_ge(ident_ok, 1)
            nc.vector.tensor_copy(sel[:], ident[0:TG, 0:TG].unsqueeze(2).broadcast_to([TG, TG, P])).then_inc(sel_ok, 1)
            dve.wait_ge(baseB_done, 1)
            nc.vector.tensor_copy(base[:], ps_small[:, 0:NG]).then_inc(baseB_ok, 1)

            def node_units(b, a, nt):
                dve.wait_ge(q_done, b + 1)
                wait(dve, q_st[a], 8 * (b - a))
                nc.vector.tensor_copy(qr[:, a, 0:nt, :], ps_q[a][:, 0:nt * H2]).then_inc(q_ok, 1)
            batches(dve, node_units)
            dve.wait_ge(w_ld2, WS)
            nc.vector.tensor_scalar(wa2h[:], wa2[:], 0.5, None, ALU.mult).then_inc(halved, 1)
            nc.vector.tensor_scalar(w2e[0:U, :], w2e[0:U, :], 0.5, None, ALU.mult).then_inc(halved, 1)
            nc.vector.tensor_scalar(wu2e[0:U, :], wu2e[0:U, :], 0.5, None, ALU.mult).then_inc(halved, 1)
            dve.wait_ge(halved, 3)
            dve.wait_ge(ww_done, 1)
            nc.vector.tensor_copy(w2T[:], ps_ww[0:U, 0:rows65]).then_inc(ww_ok, 1)
            dve.wait_ge(ww_done, 2)
            nc.vector.tensor_copy(ww[:], ps_ww[0:rows65, 0:U]).then_inc(ww_ok, 1)
            nc.vector.memset(zp[:], 0.0)
            dve.wait_ge(const_ok, 7)
            dve.wait_ge(baseB_ok, 1)

            def window(g, a):
                dve.wait_ge(ld[a], per(a, g, 32))
                T = tiles(g)
                nc.vector.tensor_scalar(rel[:, a, 0:T], dst_i[:, a, 0:T], base[:, bass.ds(g, 1)], None, ALU.subtract).then_inc(rel_ok, 1)
                dve.wait_ge(rel_ok, g + 1)
                nc.vector.tensor_reduce(rel_hi[:, bass.ds(g, 1)], rel[:, a, 0:T], AX.X, ALU.max).then_inc(ext_ok, 1)
                nc.vector.tensor_reduce(rel_lo[:, bass.ds(g, 1)], rel[:, a, 0:T], AX.X, ALU.min).then_inc(ext_ok, 1)

            def one_hots(g, a):
                T = tiles(g)
                nc.vector.tensor_tensor(hot[:, a, 0:T * WIN].rearrange("p (t n) -> p t n", t=T), iota[:, 0:WIN].unsqueeze(1).broadcast_to([P, T, WIN]),
                                        rel[:, a, 0:T].unsqueeze(2).broadcast_to([P, T, WIN]), ALU.is_equal).then_inc(hot_ok, 1)

            def add_part(g, a):
                node = dve.value_load(base_i[0:1, bass.ds(g, 1)], min_val=0, max_val=N - WIN)
                dve.wait_ge(part_done, g + 1)
                win = acc[:, bass.ds(node, WIN)]
                nc.vector.scalar_tensor_tensor(win, win, fade[0:rows65, a:a + 1], ps_part[0:rows65, 0:WIN], ALU.mult, ALU.add).then_inc(acc_ok, 1)
                nc.vector.tensor_scalar(ref[:, bass.ds(node, WIN)], ones[0:rows65, 0:WIN], neg_max[0:rows65, bass.ds(g, 1)], -1.0, ALU.mult, ALU.mult).then_inc(ref_ok, 1)
                nc.vector.scalar_tensor_tensor(zp[:], zp[:], fade[:, a:a + 1], wsum[:, a:a + 1], ALU.mult, ALU.add).then_inc(ref_ok, 1)

            def silu_logits(q, th_sem, th_count, s_sem, base_count):
                dve.wait_ge(th_sem, th_count)
                nc.vector.scalar_tensor_tensor(parts(s2, q), parts(th, q), 1.0, parts(z, q), ALU.add, ALU.mult).then_inc(s_sem, 1)
                dve.wait_ge(s_sem, base_count + 1)
                nc.vector.tensor_tensor(parts(z, q)[:, :, U:H2], parts(s2, q)[:, :, U:H2], wa2h[:].unsqueeze(1).broadcast_to([P, TQ, U]), ALU.mult).then_inc(s_sem, 1)
                dve.wait_ge(s_sem, base_count + 2)
                nc.vector.tensor_reduce(lg[:, q * TQ:(q + 1) * TQ], parts(z, q)[:, :, U:H2], AX.X, ALU.add).then_inc(s_sem, 1)

            def weigh(ws, T, a):
                nc.vector.tensor_reduce(wsum[:, a:a + 1], ws[:, 0:T], AX.X, ALU.add)
                nc.vector.tensor_copy(v[:, 0:T, U:U + 1], ws[:, 0:T].unsqueeze(2))
                return nc.vector.tensor_tensor(v[:, 0:T, 0:U], s2[:, 0:T, 0:U], ws[:, 0:T].unsqueeze(2).broadcast_to([P, T, U]), ALU.mult)

            window(0, 0)
            window(1, 1)
            one_hots(0, 0)
            dve.wait_ge(low_ok, 2)

            def add_rows(g, a, q):
                dve.wait_ge(z_done, g * NQ + q + 1)
                dve.wait_ge(gath[a][q], per(a, g, 16 * TQ))
                nc.vector.tensor_tensor(parts(z, q), ps_z[(q + a) % 2][:].rearrange("p (t u) -> p t u", t=TQ),
                                        p_rows[:, a, q * 512:(q + 1) * 512].rearrange("p (t u) -> p t u", t=TQ), ALU.add).then_inc(z_ok, 1)

            def group(g, a):
                nxt, nxt2 = following(g)
                first = isinstance(g, int) and g == 0
                T = tiles(g)
                for q in range(T // TQ):
                    if q + 1 < T // TQ:
                        add_rows(g, a, q + 1)
                    if q == (2 if nxt2 is not None else 0):
                        if nxt2 is not None:
                            window(nxt2, a)
                        elif nxt is None:
                            dve.wait_ge(ext_ok, 2 * NG)
                            chain(nc.vector.tensor_reduce(bad[:, 0:1], rel_hi[:], AX.X, ALU.max))
                            chain(nc.vector.tensor_reduce(bad[:, 1:2], rel_lo[:], AX.X, ALU.min))
                            chain(nc.vector.tensor_scalar(bad[:, 0:1], bad[:, 0:1], float(1 - WIN), None, ALU.add))
                            nc.vector.scalar_tensor_tensor(bad[:, 2:3], bad[:, 1:2], -1.0, bad[:, 0:1], ALU.mult, ALU.max).then_inc(bad_ok, 1)
                    if q == 0:
                        wait(dve, v_ok, g)
                    silu_logits(q, th_ok, g * NQ + q + 1, s_ok, (g * NQ + q) * 3)
                    if q == 1 and not first:
                        add_part(g - 1, 1 - a)
                    if q == 1:
                        if nxt is None:
                            dve.wait_ge(badT_done, 1)
                            chain(nc.vector.tensor_reduce(bad1[:, 1:2], ps_small[0:1, P:2 * P], AX.X, ALU.max))
                            chain(nc.vector.tensor_tensor(bad1[:, 2:3], bad1[:, 1:2], bad1[:, 0:1], ALU.max))
                            nc.vector.tensor_scalar(flag[:], bad1[:, 2:3], 0.0, None, ALU.is_gt).then_inc(flag_ok, 1)
                dve.wait_ge(s_ok, (g * NQ + T // TQ) * 3)
                nc.vector.tensor_scalar(lgb[:, 0:T], lg[:, 0:T], ba2c[:], None, ALU.add).then_inc(lg_ok, 1)
                dve.wait_ge(lg_ok, g + 1)
                nc.vector.tensor_reduce(pmax[:], lgb[:, 0:T], AX.X, ALU.max).then_inc(pmax_ok, 1)
                if nxt is not None:
                    one_hots(nxt, 1 - a)
                dve.wait_ge(maxT_done, g + 1)
                nc.vector.tensor_reduce(gmax[:], ps_small[0:1, 0:P], AX.X, ALU.max).then_inc(gmax_ok, 1)
                if nxt is not None:
                    add_rows(nxt, 1 - a, 0)
                dve.wait_ge(maxB_done, g + 1)
                nm = neg_max[:, bass.ds(g, 1)]
                if first:
                    nc.vector.tensor_scalar(nm, ps_small[:, 0:1], -1.0, None, ALU.mult).then_inc(negm_ok, 1)
                else:
                    nc.vector.scalar_tensor_tensor(nm, ps_small[:, 0:1], -1.0, neg_max[:, bass.ds(g - 1, 1)], ALU.mult, ALU.min).then_inc(negm_ok, 1)
                dve.wait_ge(w_ok, 2 * g + 2)
                ws = w
                if nxt is None:
                    nc.vector.tensor_tensor(wm[:, 0:T], w[:, 0:T], mask[:], ALU.mult).then_inc(wm_ok, 1)
                    dve.wait_ge(wm_ok, 1)
                    ws = wm
                weigh(ws, T, a).then_inc(v_ok, 1)
            add_rows(0, 0, 0)
            groups(dve, group)
            add_part(LAST, 0)
            dve.wait_ge(ref_ok, 2 * NG)
            nc.vector.tensor_copy(last_neg[:], neg_max[:, LAST:NG]).then_inc(low_ok, 1)

            misfit = dve.value_load(flag[0:1, 0:1], min_val=0, max_val=1)
            with dve.If(misfit == 1):
                nc.vector.memset(acc[:], 0.0).then_inc(g_acc0, 1)
                nc.vector.memset(ref[:], 0.0).then_inc(g_acc0, 1)
                nc.vector.memset(neg_max[:, 0:1], -LOW).then_inc(g_acc0, 1)
                nc.vector.memset(zp[:], 0.0).then_inc(g_acc0, 1)
                dve.wait_ge(g_acc0, 4)
                dve.wait_ge(g_step, 1)

                def group_any(g):
                    nc.vector.memset(bad[:, 0:1], 0.0).then_inc(g_start, 1)
                    k = [0]
                    per_group = NQ + 6
                    T = tiles(g)

                    def link(ins):
                        k[0] += 1
                        ins.then_inc(g_dve, 1)
                        dve.wait_ge(g_dve, g * per_group + k[0])
                    dve.wait_ge(g_gath, g * 32 * TG + 32 * T)
                    for q in range(T // TQ):
                        rows = p_rows[:, :, q * 512:(q + 1) * 512].rearrange("p a (t u) -> p a t u", t=TQ)
                        dve.wait_ge(g_z, g * NQ + q + 1)
                        link(nc.vector.tensor_tensor(parts(s2, q), ps_z[q % 2][:].rearrange("p (t u) -> p t u", t=TQ), rows[:, 0], ALU.add))
                        nc.vector.tensor_tensor(parts(z, q), parts(s2, q), rows[:, 1], ALU.add).then_inc(g_zok, 1)
                        silu_logits(q, g_th, g * NQ + q + 1, g_silu, (g * NQ + q) * 3)
                    dve.wait_ge(g_silu, (g * NQ + T // TQ) * 3)
                    link(nc.vector.tensor_scalar(lgb[:, 0:T], lg[:, 0:T], ba2c[:], None, ALU.add))
                    nc.vector.tensor_reduce(pmax[:], lgb[:, 0:T], AX.X, ALU.max).then_inc(g_pmax, 1)
                    dve.wait_ge(g_maxT, g + 1)
                    nc.vector.tensor_reduce(gmax[:], ps_small[0:1, 0:P], AX.X, ALU.max).then_inc(g_gmax, 1)
                    dve.wait_ge(g_maxB, g + 1)
                    nc.vector.scalar_tensor_tensor(neg_max[:, 1:2], ps_small[:, 0:1], -1.0, neg_max[:, 0:1], ALU.mult, ALU.min).then_inc(g_negm, 1)
                    dve.wait_ge(g_w, 2 * g + 2)
                    link(nc.vector.tensor_copy(neg_max[:, 0:1], neg_max[:, 1:2]))
                    ws = w
                    if is_last(g):
                        link(nc.vector.tensor_tensor(wm[:, 0:T], w[:, 0:T], mask[:], ALU.mult))
                        ws = wm
                    weigh(ws, T, 0).then_inc(g_v, 1)
                    dve.wait_ge(g_v, g + 1)
                    link(nc.vector.scalar_tensor_tensor(zp[:], zp[:], fade[:, 0:1], wsum[:, 0:1], ALU.mult, ALU.add))
                    link(nc.vector.tensor_scalar(acc[:], acc[:], fade[0:rows65, 0:1], None, ALU.mult))
                    link(nc.vector.tensor_copy(rel[:, 0, 0:T], dst_i[:, 0, 0:T]))
                    if not is_last(g):
                        link(nc.vector.memset(bad[:, 1:2], 0.0))
                        assert k[0] == per_group

                    def tile_sums(i, count):
                        nc.vector.tensor_scalar(rel[:, 1, 0:T], rel[:, 0, 0:T], tile0[:, bass.ds(i, 1)], None, ALU.subtract).then_inc(g_rel, 1)
                        dve.wait_ge(g_rel, count + 1)
                        nc.vector.tensor_tensor(hot_g[:, 0:T, :], iota[:].unsqueeze(1).broadcast_to([P, T, P]),
                                                rel[:, 1, 0:T].unsqueeze(2).broadcast_to([P, T, P]), ALU.is_equal).then_inc(g_hot, 1)
                        dve.wait_ge(g_part, count + 1)
                        cols = acc[:, bass.ds(i * P, P)]
                        nc.vector.tensor_tensor(cols, cols, ps_part[0:rows65, 0:P], ALU.add).then_inc(g_acc, 1)
                        dve.wait_ge(g_acc, count + 1)
                    dve.sem_inc(turn, 1)
                    with dve.Fori(0, NT) as i:
                        tile_sums(i, g * NT + i)
                group_any(0)
                with dve.Fori(1, LAST) as g:
                    group_any(g)
                group_any(LAST)
                nc.vector.tensor_scalar(ref[:], ref[:], neg_max[0:rows65, 0:1], None, ALU.subtract).then_inc(g_acc0, 1)
                nc.vector.tensor_copy(last_neg[:], neg_max[:, 0:1]).then_inc(g_acc0, 1)
                dve.wait_ge(g_acc0, 6)
            dve.wait_ge(low_ok, 3)
            dve.sem_inc(sums_ok, 1)
            dve.wait_ge(zall_done, 1)
            nc.vector.tensor_copy(zall[:], ps_small[:, 0:1]).then_inc(zall_ok, 1)
            dve.wait_ge(zall_ok, 1)
            nc.vector.reciprocal(rz[:], zall[:]).then_inc(rz_ok, 1)
            dve.wait_ge(rz_ok, 1)
            nc.vector.tensor_scalar(wws[:], ww[:], rz[0:rows65, :], None, ALU.mult).then_inc(scale_ok, 1)

            def rescale(b, a, nt):
                dve.wait_ge(refx_ok, b + 1)
                c = bass.ds(b * NBT * P, nt * P)
                nc.vector.tensor_tensor(acc[:, c], acc[:, c], ref[:, c], ALU.mult).then_inc(scaled_ok, 1)

            def whole_u(b, a, nt):
                dve.wait_ge(u_done, b + 1)
                c = bass.ds(b * NBT * P, nt * P)
                nc.vector.tensor_tensor(hT[0:U, c], hT[0:U, c], ps_u[a][0:U, 0:nt * P], ALU.add).then_inc(u_ok, 1)

            def whole_y(b, a, nt):
                dve.wait_ge(y_done, b + 1)
                wait(dve, out_st[a], 8 * (b - a))
                nc.vector.tensor_tensor(y[:, a, 0:nt, :], ps_y[a][:, 0:nt * D].rearrange("p (t d) -> p t d", t=nt),
                                        x_sb[:, bass.ds(b * NBT, nt), :], ALU.add).then_inc(y_ok, 1)

            def update(b, a, nt):
                if nodes_of(b, 2):
                    rescale(b + 2, a, nodes_of(b, 2))
                if nodes_of(b, 1):
                    whole_u(b + 1, 1 - a, nodes_of(b, 1))
                dve.wait_ge(thu_ok, b + 1)
                wait(dve, y_done, b - 1)
                nc.vector.scalar_tensor_tensor(su[0:U, a, 0:nt * P], thu[:, a, 0:nt * P], 1.0, hT[0:U, bass.ds(b * NBT * P, nt * P)],
                                               ALU.add, ALU.mult).then_inc(su_ok, 1)
                if not (isinstance(b, int) and b == 0):
                    whole_y(b - 1, 1 - a, NBT)
            rescale(0, 0, NBT)
            rescale(1, 1, NBT)
            whole_u(0, 0, NBT)
            batches(dve, update)
            whole_y(NB, 0, 1)
_INS = ["x", "src", "dst", "edge_attr_32"] + ["L0_gnn_" + n for n in
        ("W1", "b1", "W2", "b2", "Wa1", "ba1", "Wa2", "ba2", "Wu1", "bu1", "Wu2", "bu2")]


def kernel(**inputs):
    import numpy as np
    import concourse.bacc as bacc
    from concourse.bass_utils import run_bass_kernel_spmd

    nc = bacc.Bacc("TRN2", target_bir_lowering=False, num_devices=1)
    arrays, args = {}, []
    for name in _INS:
        a = np.ascontiguousarray(inputs[name])
        arrays[name] = a
        args.append(nc.dram_tensor(name, a.shape, mybir.dt.from_np(a.dtype), kind="ExternalInput").ap())
    args.append(nc.dram_tensor("out", inputs["x"].shape, F32, kind="ExternalOutput").ap())
    build(nc, *args)
    r = run_bass_kernel_spmd(nc, [arrays], core_ids=[0])
    return r.results[0]["out"]
```

```python
import concourse.bass as bass
from concourse import mybir
from contextlib import ExitStack

F32 = mybir.dt.float32
BF16 = mybir.dt.bfloat16
I32 = mybir.dt.int32
ALU = mybir.AluOpType
ACT = mybir.ActivationFunctionType
AX = mybir.AxisListType


def build(nc, x, src, dst, ef, W1, b1, W2, b2, Wa1, ba1, Wa2, ba2, Wu1, bu1, Wu2, bu2, out):
    N, D = x.shape
    E, DE = ef.shape
    U = W2.shape[0]
    P = 128
    H2 = 2 * U
    U1 = U + 1
    TG = 20
    GE = TG * P
    NG = -(-E // GE)
    LAST = NG - 1
    TQ = 4
    NQ = TG // TQ
    TL = -(-(E - LAST * GE) // (TQ * P)) * TQ
    DUP = LAST * GE + TL * P - E
    WIN = P - DE
    NT = -(-N // P)
    NP = NT * P
    LT = N - (NT - 1) * P
    NBT = 4
    NB = NT // NBT
    NU = (NB + 2) // 2 * 2
    assert NT == NB * NBT + 1 and NB < NU < LAST - 2 and NBT % 2 == 0 and NG % 2 == 1 and NB % 2 == 0
    assert H2 == P and 2 * D == P and U == D and DE * TQ == P
    PIECES = [(0, NT // 3), (NT // 3, 2 * NT // 3), (2 * NT // 3, NT)]
    EPS = 1e-5
    LOW = -3.0e38

    p_tab = nc.dram_tensor("p_tab", (N, H2), F32).ap()
    q_tab = nc.dram_tensor("q_tab", (N, H2), F32).ap()

    ctx = ExitStack()
    with ctx:
        def sb(name, shape, dt=F32):
            return ctx.enter_context(nc.sbuf_tensor(name, shape, dt))

        def sem(name):
            return ctx.enter_context(nc.semaphore(name))

        def flat(t):
            return t[:].rearrange("p a b -> p (a b)")

        ident = sb("ident", [P, P])
        iota = sb("iota", [P, P])
        row_no = sb("row_no", [P, 1])
        ones = sb("ones", [P, P])
        tile0 = sb("tile0", [P, NT])
        mask = sb("mask", [P, TL])
        sel = sb("sel", [TG, TG, P], BF16)
        w_p = sb("w_p", [P, H2])
        w_q = sb("w_q", [D + 1, H2])
        wa2 = sb("wa2", [P, U])
        wa2h = sb("wa2h", [P, U])
        ba2c = sb("ba2c", [P, 1])
        w2e = sb("w2e", [U1, U])
        wu1h = sb("wu1h", [D + 1, U])
        wu1a = sb("wu1a", [U, U])
        wu2e = sb("wu2e", [U1, D])
        x_sb = sb("x_sb", [P, NT, D])
        hT = sb("hT", [D + 1, NU * NBT * P])
        stat = sb("stat", [P, 6, NT])
        first_i = sb("first_i", [1, NG], I32)
        first_f = sb("first_f", [1, NG])
        base_f = sb("base_f", [1, NG])
        base_i = sb("base_i", [1, NG], I32)
        base = sb("base", [P, NG])
        rel_hi = sb("rel_hi", [P, NG])
        rel_lo = sb("rel_lo", [P, NG])
        back = sb("back", [1, NG])
        bad = sb("bad", [P, 3])
        last_neg = sb("last_neg", [P, 1])
        wsum = sb("wsum", [P, 2])
        zp = sb("zp", [P, 1])
        w2T = sb("w2T", [U, U1])
        ww = sb("ww", [U1, U])
        wws = sb("wws", [U1, U])
        bad1 = sb("bad1", [1, 4])
        flag = sb("flag", [1, 1], I32)
        src_i = sb("src_i", [P, 2, TG], I32)
        dst_i = sb("dst_i", [P, 2, TG], I32)
        ef_sb = sb("ef_sb", [P, 2, TG * DE])
        q_win = sb("q_win", [P, 2, H2])
        p_rows = sb("p_rows", [P, 2, TG * H2])
        rel = sb("rel", [P, 2, TG])
        relT = sb("relT", [TG, P], BF16)
        hot = sb("hot", [P, 2, TG * WIN])
        comb = sb("comb", [P, 2, TG * P])
        z = sb("z", [P, TG, H2])
        th = sb("th", [P, TG, H2])
        s2 = sb("s2", [P, TG, H2])
        lg = sb("lg", [P, TG])
        lgb = sb("lgb", [P, TG])
        pmax = sb("pmax", [P, 1])
        gmax = sb("gmax", [1, 1])
        neg_max = sb("neg_max", [P, NG])
        fade = sb("fade", [P, 2])
        w = sb("w", [P, TG])
        wm = sb("wm", [P, TG])
        v = sb("v", [P, TG, U1])
        acc = sb("acc", [U1, NP])
        ref = sb("ref", [U1, NP])
        zall = sb("zall", [P, 1])
        rz = sb("rz", [P, 1])
        su = sb("su", [U1, 2, NBT * P])
        h_p = flat(z)[:, 0:NBT * P].rearrange("p (a n) -> p a n", a=2)
        h_q = flat(z)[0:D + 1, 2 * NBT * P:4 * NBT * P].rearrange("p (a n) -> p a n", a=2)
        pr, qr = (flat(th)[:, k * NBT * H2:(k + 2) * NBT * H2].rearrange("p (a t u) -> p a t u", a=2, t=NBT) for k in (0, 2))
        xc = flat(p_rows)[:, 0:NT * D].rearrange("p (t d) -> p t d", d=D)
        sq = flat(comb)[:, 0:NT * D].rearrange("p (t d) -> p t d", d=D)
        hn = flat(comb)[:, NT * D:(NT + 2 * NBT) * D].rearrange("p (a t d) -> p a t d", a=2, t=NBT)
        thu = flat(th)[0:U, 0:2 * NBT * P].rearrange("p (a n) -> p a n", a=2)
        y = flat(s2)[:, 0:2 * NBT * D].rearrange("p (a t d) -> p a t d", a=2, t=NBT)
        hot_g = flat(hot)[:, 0:TG * P].rearrange("p (t n) -> p t n", t=TG)

        bank = [ctx.enter_context(nc.psum_tensor(f"bank{i}", [P, 512], F32)) for i in range(6)]
        ps_prep = ctx.enter_context(nc.psum_tensor("ps_prep", [P, 1024], F32))
        ps_relT = ps_prep[0:TG, TG * DE:TG * DE + P]
        ps_row = bank[0:2]
        ps_z = bank[2:4]
        ps_part = bank[4]
        ps_small = bank[5]
        ps_hT = bank[0:2]
        ps_p = [[bank[2], bank[3]], [bank[4], ps_prep]]
        ps_q = [bank[4], ps_prep[:, 0:512]]
        ps_ww = bank[5]
        ps_u = bank[2:4]
        ps_y = [bank[4], ps_prep[:, 0:512]]

        (zeroed, ident_ok, const_ok, sel_ok, w_ld, w_ld2, first_ld, halved, low_ok, dve_step) = (
            sem(n) for n in ("zeroed", "ident_ok", "const_ok", "sel_ok", "w_ld", "w_ld2", "first_ld", "halved", "low_ok", "dve_step"))
        xc_ok, sq_ok, std_ok, ww_done, ww_ok, scale_ok = (
            sem(n) for n in ("xc_ok", "sq_ok", "std_ok", "ww_done", "ww_ok", "scale_ok"))
        x_ld = [sem(f"x_ld{h}") for h in range(len(PIECES))]
        (base_ok, baseB_done, baseB_ok, var_ok, rstd_ok, hn_ok, hT_done, hst_ok, hT_ok, p_done, p_ok, hq_ok, q_done, q_ok, uh_done, uh_ok) = (
            sem(n) for n in ("base_ok", "baseB_done", "baseB_ok", "var_ok", "rstd_ok", "hn_ok", "hT_done", "hst_ok", "hT_ok",
                             "p_done", "p_ok", "hq_ok", "q_done", "q_ok", "uh_done", "uh_ok"))
        p_st = [sem("p_st0"), sem("p_st1")]
        q_st = [sem("q_st0"), sem("q_st1")]
        ld = [sem("ld0"), sem("ld1")]
        src_ld = [sem("src_ld0"), sem("src_ld1")]
        win_ld = [sem("win_ld0"), sem("win_ld1")]
        gath = [[sem(f"gath{a}{q}") for q in range(NQ)] for a in range(2)]
        (rel_ok, hot_ok, prep_done, efT_ok, relT_ok, row_done, abs_ok, comb_ok) = (
            sem(n) for n in ("rel_ok", "hot_ok", "prep_done", "efT_ok", "relT_ok", "row_done", "abs_ok", "comb_ok"))
        (z_done, z_ok, th_ok, s_ok, lg_ok, pmax_ok, maxT_done, gmax_ok, maxB_done, negm_ok) = (
            sem(n) for n in ("z_done", "z_ok", "th_ok", "s_ok", "lg_ok", "pmax_ok", "maxT_done",
                             "gmax_ok", "maxB_done", "negm_ok"))
        (w_ok, wm_ok, v_ok, part_done, acc_ok, ref_ok) = (
            sem(n) for n in ("w_ok", "wm_ok", "v_ok", "part_done", "acc_ok", "ref_ok"))
        (bad_ok, badT_done, flag_ok) = (sem(n) for n in ("bad_ok", "badT_done", "flag_ok"))
        (sums_ok, refx_ok, scaled_ok, zall_done, zall_ok, rz_ok) = (
            sem(n) for n in ("sums_ok", "refx_ok", "scaled_ok", "zall_done", "zall_ok", "rz_ok"))
        (u_done, u_ok, thu_ok, su_ok, y_done, y_ok) = (
            sem(n) for n in ("u_done", "u_ok", "thu_ok", "su_ok", "y_done", "y_ok"))
        out_st = [sem("out_st0"), sem("out_st1")]
        (g_start, g_ld, g_gath, g_prep, g_efT, g_z, g_zok, g_th, g_pmax, g_maxT, g_gmax, g_maxB, g_negm, g_w, g_v, g_hot, g_part,
         g_acc, g_step) = (
            sem("g_" + n) for n in ("start", "ld", "gath", "prep", "efT", "z", "zok", "th", "pmax", "maxT", "gmax", "maxB", "negm",
                                    "w", "v", "hot", "part", "acc", "step"))
        turn = sem("turn")
        ext_ok, g_acc0, g_dve, g_silu, g_rel = sem("ext_ok"), sem("g_acc0"), sem("g_dve"), sem("g_silu"), sem("g_rel")

        def wait(eng, s, n):
            if not (isinstance(n, int) and n <= 0):
                eng.wait_ge(s, n)

        def groups(eng, body, early=None):
            for g in range(2):
                (early or body)(g, g)
            if early:
                with eng.Fori(1, NU // 2) as pair:
                    early(pair * 2, 0)
                    early(pair * 2 + 1, 1)
            with eng.Fori(NU // 2 if early else 1, LAST // 2 - 1) as pair:
                body(pair * 2, 0)
                body(pair * 2 + 1, 1)
            body(LAST - 2, 0)
            body(LAST - 1, 1)
            body(LAST, 0)

        def batches(eng, body):
            body(0, 0, NBT)
            body(1, 1, NBT)
            with eng.Fori(1, NB // 2 - 1) as pair:
                body(pair * 2, 0, NBT)
                body(pair * 2 + 1, 1, NBT)
            body(NB - 2, 0, NBT)
            body(NB - 1, 1, NBT)
            body(NB, 0, 1)

        def is_last(g):
            return isinstance(g, int) and g == LAST

        def following(g):
            return tuple(g + k if not isinstance(g, int) or g + k <= LAST else None for k in (1, 2))

        def tiles(g):
            return TL if is_last(g) else TG

        def edge0(g):
            return E - TL * P if is_last(g) else g * GE

        def per(a, g, n):
            return (g - a) * (n // 2) + n

        def stored(eng, st):
            eng.wait_ge(st[0], 16 * (NB // 2 + 1))
            eng.wait_ge(st[1], 16 * (NB // 2))

        def nodes_of(b, ahead):
            if not isinstance(b, int) or b + ahead < NB:
                return NBT
            return 1 if b + ahead == NB else 0

        def parts(t, q):
            return t[:, q * TQ:(q + 1) * TQ, :]

        def load_src(eng, g, a, s):
            e0, T = edge0(g), tiles(g)
            eng.dma_start(src_i[:, a, 0:T], src[bass.ds(e0, T * P)].rearrange("(p t) -> p t", t=T)).then_inc(s, 16)

        def load_edges(eng, g, a, s):
            e0, T = edge0(g), tiles(g)
            eng.dma_start(dst_i[:, a, 0:T], dst[bass.ds(e0, T * P)].rearrange("(p t) -> p t", t=T)).then_inc(s, 16)
            eng.dma_start(ef_sb[:, a, 0:T * DE], ef[bass.ds(e0, T * P), :].rearrange("(p t) f -> p (t f)", t=T)).then_inc(s, 16)

        x_t = x[0:(NT - 1) * P, :].rearrange("(t p) d -> p t d", p=P)
        p_t = p_tab[0:(NT - 1) * P, :].rearrange("(t p) d -> p t d", p=P)
        q_t = q_tab[0:(NT - 1) * P, :].rearrange("(t p) d -> p t d", p=P)
        out_t = out[0:(NT - 1) * P, :].rearrange("(t p) d -> p t d", p=P)
        WS = 16 * (2 * 2 + 9)

        block = ctx.enter_context(nc.Block())

        @block.sync
        def _(sp):
            for h, (t0, t1) in enumerate(PIECES):
                t1 = min(t1, NT - 1)
                sp.dma_start(x_sb[:, t0:t1, :], x_t[:, t0:t1, :]).then_inc(x_ld[h], 16)
            sp.wait_ge(zeroed, 1)
            sp.dma_start(x_sb[0:LT, NT - 1, :], x[(NT - 1) * P:N, :]).then_inc(x_ld[-1], 16)
            with nc.allow_non_contiguous_dma(reason="one dst of each group"):
                sp.dma_start(first_i[:, 0:LAST], dst[0:LAST * GE].rearrange("(a g e) -> a g e", a=1, e=GE)[:, :, 0]).then_inc(first_ld, 16)
            sp.dma_start(first_i[:, LAST:NG], dst[E - TL * P:E - TL * P + 1][None, :]).then_inc(first_ld, 16)
            for a in range(2):
                sp.dma_start(q_win[WIN:P, a, 0:U], W1[2 * D:2 * D + DE, :]).then_inc(w_ld2, 16)
                sp.dma_start(q_win[WIN:P, a, U:H2], Wa1[2 * D:2 * D + DE, :]).then_inc(w_ld2, 16)

            def load_group(g, a):
                wait(sp, prep_done, g - 1)
                load_edges(sp, g, a, ld[a])
                if not (isinstance(g, int) and g < 2):
                    sp.wait_ge(gath[a][NQ - 1], per(a, g - 2, 16 * TQ))
                load_src(sp, g, a, src_ld[a])
            load_group(0, 0)
            load_group(1, 1)
            sp.dma_start(wa2[:], Wa2.rearrange("a b -> b a").broadcast_to([P, U])).then_inc(w_ld2, 16)
            sp.dma_start(ba2c[:], ba2[None, :].broadcast_to([P, 1])).then_inc(w_ld2, 16)
            sp.dma_start(w2e[0:U, :], W2).then_inc(w_ld2, 16)
            sp.dma_start(w2e[U:U1, :], b2[None, :]).then_inc(w_ld2, 16)
            sp.dma_start(wu1h[0:D, :], Wu1[0:D, :]).then_inc(w_ld2, 16)
            sp.dma_start(wu1h[D:D + 1, :], bu1[None, :]).then_inc(w_ld2, 16)
            sp.dma_start(wu1a[:], Wu1[D:D + U, :]).then_inc(w_ld2, 16)
            sp.dma_start(wu2e[0:U, :], Wu2).then_inc(w_ld2, 16)
            sp.dma_start(wu2e[U:U1, :], bu2[None, :]).then_inc(w_ld2, 16)

            def store_rows(tab, tab_t, rows, rows_ok, st):
                def store(b, a, nt):
                    sp.wait_ge(rows_ok, b + 1)
                    if nt > 1:
                        sp.dma_start(tab_t[:, bass.ds(b * NBT, NBT), :], rows[:, a, :, :]).then_inc(st[a], 16)
                    else:
                        sp.dma_start(tab[(NT - 1) * P:N, :], rows[0:LT, a, 0, :]).then_inc(st[a], 16)
                return store
            batches(sp, store_rows(p_tab, p_t, pr, p_ok, p_st))
            batches(sp, store_rows(q_tab, q_t, qr, q_ok, q_st))
            groups(sp, lambda g, a: None if isinstance(g, int) and g < 2 else load_group(g, a))

            def store_out(b, a, nt):
                sp.wait_ge(y_ok, b + 1)
                if nt > 1:
                    sp.dma_start(out_t[:, bass.ds(b * NBT, NBT), :], y[:, a, :, :]).then_inc(out_st[a], 16)
                else:
                    sp.dma_start(out[(NT - 1) * P:N, :], y[0:LT, a, 0, :]).then_inc(out_st[a], 16)
            batches(sp, store_out)
            sp.wait_ge(out_st[0], 16 * (NB // 2 + 1))
            sp.wait_ge(out_st[1], 16 * (NB // 2))

        @block.gpsimd
        def _(pool):
            nc.gpsimd.memset(x_sb[:, NT - 1, :], 0.0).then_inc(zeroed, 1)
            nc.gpsimd.memset(ones[:], 1.0).then_inc(const_ok, 1)
            nc.gpsimd.memset(ident[:], 0.0).then_inc(zeroed, 1)
            nc.gpsimd.memset(mask[:], 0.0).then_inc(zeroed, 1)
            nc.gpsimd.iota(iota[:], [[1, P]], base=0, channel_multiplier=0, allow_small_or_imprecise_dtypes=True).then_inc(const_ok, 1)
            nc.gpsimd.iota(row_no[:], [[0, 1]], base=0, channel_multiplier=-1, allow_small_or_imprecise_dtypes=True).then_inc(const_ok, 1)
            pool.wait_ge(zeroed, 3)
            nc.gpsimd.affine_select(out=ident[:], in_=ident[:], compare_op=ALU.not_equal, fill=1.0,
                                    base=0, pattern=[[-1, P]], channel_multiplier=1).then_inc(ident_ok, 1)
            nc.gpsimd.affine_select(out=mask[:], in_=mask[:], compare_op=ALU.is_gt, fill=1.0,
                                    base=DUP, pattern=[[-1, TL]], channel_multiplier=-TL).then_inc(const_ok, 1)
            pool.wait_ge(ident_ok, 1)
            pool.wait_ge(const_ok, 4)
            nc.gpsimd.memset(h_q[D:D + 1, :, :], 1.0).then_inc(const_ok, 1)
            pool.wait_ge(const_ok, 5)
            nc.gpsimd.memset(hT[D:D + 1, 0:NP], 1.0).then_inc(const_ok, 1)
            pool.wait_ge(const_ok, 6)
            nc.gpsimd.memset(hT[:, NP:], 1.0).then_inc(const_ok, 1)
            pool.wait_ge(const_ok, 7)
            nc.gpsimd.memset(su[U:U1, :, :], 1.0).then_inc(const_ok, 1)
            pool.wait_ge(const_ok, 8)
            nc.gpsimd.memset(acc[:], 0.0).then_inc(low_ok, 1)
            nc.gpsimd.memset(ref[:], LOW).then_inc(low_ok, 1)
            stored(pool, p_st)

            def gather(g, a):
                pool.wait_ge(src_ld[a], per(a, g, 16))
                for q in range(tiles(g) // TQ):
                    if not (isinstance(g, int) and g < 2):
                        pool.wait_ge(z_ok, (g - 2) * NQ + q + 1)
                        pool.sem_inc(turn, 1)
                    for t in range(q * TQ, (q + 1) * TQ):
                        pool.indirect_dma_start(p_rows[:, a, t * H2:(t + 1) * H2], None, p_tab,
                                                bass.IndirectOffsetOnAxis(src_i[:, a, t:t + 1], 0)).then_inc(gath[a][q], 16)
            groups(pool, gather)

            stored(pool, q_st)
            pool.wait_ge(flag_ok, 1)
            misfit = pool.value_load(flag[0:1, 0:1], min_val=0, max_val=1)
            with pool.If(misfit == 1):
                nc.gpsimd.iota(tile0[:], [[P, NT]], base=0, channel_multiplier=0,
                               allow_small_or_imprecise_dtypes=True).then_inc(g_step, 1)

                def gather_all(g):
                    pool.wait_ge(g_start, g + 1)
                    load_src(pool, g, 0, g_ld)
                    load_edges(pool, g, 0, g_ld)
                    pool.wait_ge(g_ld, (g + 1) * 48)
                    pool.sem_inc(turn, 1)
                    for t in range(tiles(g)):
                        pool.indirect_dma_start(p_rows[:, 0, t * H2:(t + 1) * H2], None, p_tab,
                                                bass.IndirectOffsetOnAxis(src_i[:, 0, t:t + 1], 0)).then_inc(g_gath, 16)
                        pool.indirect_dma_start(p_rows[:, 1, t * H2:(t + 1) * H2], None, q_tab,
                                                bass.IndirectOffsetOnAxis(dst_i[:, 0, t:t + 1], 0)).then_inc(g_gath, 16)
                gather_all(0)
                with pool.Fori(1, LAST) as g:
                    gather_all(g)
                gather_all(LAST)

        @block.scalar
        def _(act):
            for j in range(2):
                act.dma_start(w_p[j * D:(j + 1) * D, 0:U], W1[0:D, :]).then_inc(w_ld, 16)
                act.dma_start(w_p[j * D:(j + 1) * D, U:H2], Wa1[0:D, :]).then_inc(w_ld, 16)
            act.dma_start(w_q[0:D, 0:U], W1[D:2 * D, :]).then_inc(w_ld, 16)
            act.dma_start(w_q[0:D, U:H2], Wa1[D:2 * D, :]).then_inc(w_ld, 16)
            act.dma_start(w_q[D:D + 1, 0:U], b1[None, :]).then_inc(w_ld, 16)
            act.dma_start(w_q[D:D + 1, U:H2], ba1[None, :]).then_inc(w_ld, 16)
            for h, (t0, t1) in enumerate(PIECES):
                act.wait_ge(xc_ok, h + 1)
                nc.scalar.activation(sq[:, t0:t1, :], xc[:, t0:t1, :], ACT.Square).then_inc(sq_ok, 1)
            act.wait_ge(var_ok, len(PIECES))
            nc.scalar.activation(stat[:, 3, :], stat[:, 0, :], ACT.Sqrt).then_inc(std_ok, 1)

            def node_rows(b, a, nt):
                n = -(-nt // 2) * P
                act.wait_ge(hT_done, b + 1)
                wait(act, p_done, b - 1)
                nc.scalar.activation(h_p[:, a, 0:n], ps_hT[a][:, 0:n], ACT.Relu).then_inc(hst_ok, 1)
                cols = hT[0:D, bass.ds(b * NBT * P, nt * P)]
                if nt > 1:
                    cols = cols.rearrange("p (k j n) -> p k j n", j=2, n=P)
                    nc.scalar.activation(cols[:, :, 1, :], ps_hT[a][D:P, 0:n].rearrange("p (k n) -> p k n", n=P), ACT.Relu)
                    cols = cols[:, :, 0, :]
                    nc.scalar.activation(cols, ps_hT[a][0:D, 0:n].rearrange("p (k n) -> p k n", n=P), ACT.Relu).then_inc(hT_ok, 1)
                else:
                    nc.scalar.activation(cols, ps_hT[a][0:D, 0:n], ACT.Relu).then_inc(hT_ok, 1)
            batches(act, node_rows)

            def copy_h(b, a, nt):
                wait(act, q_done, b - 1)
                act.sem_inc(turn, 1)
                nc.scalar.activation(h_q[0:D, a, 0:nt * P], hT[0:D, bass.ds(b * NBT * P, nt * P)], ACT.Copy).then_inc(hq_ok, 1)

            act.wait_ge(hT_ok, NB + 1)
            batches(act, copy_h)

            def window(g, a):
                wait(act, z_done, (g - 1) * NQ)
                node = act.value_load(base_i[0:1, bass.ds(g, 1)], min_val=0, max_val=N - WIN)
                act.dma_start(q_win[0:WIN, a, :], q_tab[bass.ds(node, WIN), :]).then_inc(win_ld[a], 16)

            def copy_efT(dst_a, T):
                for j in range(TQ):
                    last = nc.scalar.copy(comb[WIN:P, dst_a, 0:T * P].rearrange("p (q j e) -> p q j e", j=TQ, e=P)[:, :, j, :],
                                          ps_prep[j * DE:(j + 1) * DE, 0:T * DE].rearrange("p (q e) -> p q e", e=P))
                return last

            def copy_relT(g, a):
                act.wait_ge(prep_done, g + 1)
                wait(act, row_done, g * NQ)
                nc.scalar.copy(relT[0:tiles(g), :], ps_relT[0:tiles(g), :]).then_inc(relT_ok, 1)

            def one_hots(g, a, qs):
                qs = [q for q in qs if q < tiles(g) // TQ]
                for q in qs:
                    bank_q = ps_row[(q + a) % 2][0:WIN, :]
                    act.wait_ge(row_done, g * NQ + q + 1)
                    nc.scalar.activation(bank_q, bank_q, ACT.Abs, bias=row_no[0:WIN, :]).then_inc(abs_ok, 1)
                for q in qs:
                    act.wait_ge(abs_ok, g * NQ + q + 1)
                    nc.scalar.activation(comb[0:WIN, a, q * 512:(q + 1) * 512], ps_row[(q + a) % 2][0:WIN, :], ACT.Relu,
                                         scale=-1.0, bias=ones[0:WIN, 0:1]).then_inc(comb_ok, 1)

            stored(act, q_st)
            act.wait_ge(base_ok, 1)
            act.wait_ge(const_ok, 8)
            window(0, 0)
            copy_relT(0, 0)
            copy_efT(0, TG).then_inc(efT_ok, 1)
            for qs in ([0, 1], [2, 3], [4]):
                one_hots(0, 0, qs)
            copy_relT(1, 1)

            def group(g, a, units=False):
                nxt, nxt2 = following(g)
                if nxt is not None:
                    window(nxt, 1 - a)
                for q in range(tiles(g) // TQ):
                    act.wait_ge(z_ok, g * NQ + q + 1)
                    nc.scalar.activation(parts(th, q), parts(z, q), ACT.Tanh, scale=0.5).then_inc(th_ok, 1)
                    if nxt is not None:
                        if q == 1:
                            copy_efT(1 - a, tiles(nxt)).then_inc(efT_ok, 1)
                        one_hots(nxt, 1 - a, {0: [0, 1], 2: [2], 4: [3, 4]}.get(q, []))
                act.wait_ge(negm_ok, g + 1)
                nm = neg_max[:, bass.ds(g, 1)]
                nc.scalar.activation(w[:, 0:tiles(g)], lgb[:, 0:tiles(g)], ACT.Exp, bias=nm).then_inc(w_ok, 1)
                if not (isinstance(g, int) and g == 0):
                    nc.scalar.activation(fade[:, a:a + 1], neg_max[:, bass.ds(g - 1, 1)], ACT.Exp, scale=-1.0, bias=nm).then_inc(w_ok, 1)
                else:
                    nc.scalar.activation(fade[:, a:a + 1], row_no[:], ACT.Exp).then_inc(w_ok, 1)
                if nxt2 is not None:
                    copy_relT(nxt2, a)
                if units:
                    act.wait_ge(uh_done, g + 1)
                    act.sem_inc(turn, 1)
                    nc.scalar.activation(hT[0:U, bass.ds(g * NBT * P, NBT * P)], ps_row[a][0:U, :], ACT.Copy).then_inc(uh_ok, 1)
            groups(act, group, early=lambda g, a: group(g, a, units=True))

            act.wait_ge(flag_ok, 1)
            misfit = act.value_load(flag[0:1, 0:1], min_val=0, max_val=1)
            with act.If(misfit == 1):
                def group_any(g):
                    act.wait_ge(g_prep, g + 1)
                    copy_efT(0, tiles(g)).then_inc(g_efT, 1)
                    for q in range(tiles(g) // TQ):
                        act.wait_ge(g_zok, g * NQ + q + 1)
                        nc.scalar.activation(parts(th, q), parts(z, q), ACT.Tanh, scale=0.5).then_inc(g_th, 1)
                    act.wait_ge(g_negm, g + 1)
                    nc.scalar.activation(w[:, 0:tiles(g)], lgb[:, 0:tiles(g)], ACT.Exp, bias=neg_max[:, 1:2]).then_inc(g_w, 1)
                    nc.scalar.activation(fade[:, 0:1], neg_max[:, 0:1], ACT.Exp, scale=-1.0, bias=neg_max[:, 1:2]).then_inc(g_w, 1)
                group_any(0)
                with act.Fori(1, LAST) as g:
                    group_any(g)
                group_any(LAST)

            act.wait_ge(sums_ok, 1)

            def fade_ref(b, a, nt):
                c = bass.ds(b * NBT * P, nt * P)
                nc.scalar.activation(ref[:, c], ref[:, c], ACT.Exp, bias=last_neg[0:U1, :]).then_inc(refx_ok, 1)

            def update(b, a, nt):
                n = nt * P
                if nodes_of(b, 2):
                    fade_ref(b + 2, a, nodes_of(b, 2))
                act.wait_ge(u_ok, b + 1)
                wait(act, su_ok, b - 1)
                act.sem_inc(turn, 1)
                nc.scalar.activation(thu[:, a, 0:n], hT[0:U, bass.ds(b * NBT * P, n)], ACT.Tanh, scale=0.5).then_inc(thu_ok, 1)
            for b in range(2):
                fade_ref(b, b % 2, NBT)
            batches(act, update)

        @block.tensor
        def _(pe):
            pe.wait_ge(ident_ok, 1)
            pe.wait_ge(w_ld, 128)

            def transpose_rows(b, a, nt):
                pe.wait_ge(hn_ok, b + 1)
                wait(pe, hT_ok, b - 1)
                pe.sem_inc(turn, 1)
                for k in range(-(-nt // 2)):
                    pair = hn[:, a, 2 * k:2 * k + 2, :].rearrange("p t d -> p (t d)")
                    last = nc.tensor.transpose(ps_hT[a][:, k * P:(k + 1) * P], pair, ident[:])
                last.then_inc(hT_done, 1)

            def node_rows(b, a, nt):
                if nodes_of(b, 1):
                    transpose_rows(b + 1, 1 - a, nodes_of(b, 1))
                pe.wait_ge(hst_ok, b + 1)
                wait(pe, p_ok, b - 1)
                for t in range(nt):
                    k, rows = t // 2, slice(t % 2 * D, (t % 2 + 1) * D)
                    last = nc.tensor.matmul(ps_p[a][t % 2][:, k * H2:(k + 1) * H2], h_p[rows, a, k * P:(k + 1) * P], w_p[rows, :], start=True, stop=True)
                last.then_inc(p_done, 1)
            transpose_rows(0, 0, NBT)
            batches(pe, node_rows)
            pe.wait_ge(const_ok, 8)
            pe.wait_ge(base_ok, 1)
            nc.tensor.matmul(ps_small[:, 0:NG], ones[0:1, :], base_f[:], start=True, stop=True).then_inc(baseB_done, 1)
            pe.wait_ge(w_ld2, WS)

            pe.wait_ge(p_ok, NB + 1)

            def q_rows(b, a, nt):
                pe.wait_ge(hq_ok, b + 1)
                wait(pe, q_ok, b - 1)
                for t in range(nt):
                    last = nc.tensor.matmul(ps_q[a][:, t * H2:(t + 1) * H2], h_q[:, a, t * P:(t + 1) * P], w_q[:], start=True, stop=True)
                last.then_inc(q_done, 1)
            batches(pe, q_rows)
            pe.wait_ge(baseB_ok, 1)
            pe.wait_ge(sel_ok, 1)
            pe.wait_ge(hT_ok, NB + 1)
            pe.wait_ge(q_ok, NB + 1)
            pe.wait_ge(halved, 3)
            nc.tensor.transpose(ps_ww[0:U, 0:U1], w2e[:], ident[0:U1, 0:U1]).then_inc(ww_done, 1)
            pe.wait_ge(ww_ok, 1)
            nc.tensor.matmul(ps_ww[0:U1, 0:U], w2T[:], wu1a[:], start=True, stop=True).then_inc(ww_done, 1)
            pe.wait_ge(ww_ok, 2)

            def transpose_ef(a, T):
                for q in range(T // TQ):
                    last = nc.tensor.transpose(ps_prep[:, q * P:(q + 1) * P], ef_sb[:, a, q * P:(q + 1) * P], ident[:])
                return last

            def prepare(g, a):
                pe.wait_ge(rel_ok, g + 1)
                pe.wait_ge(ld[a], per(a, g, 32))
                wait(pe, efT_ok, g)
                pe.sem_inc(turn, 1)
                transpose_ef(a, tiles(g))
                nc.tensor.transpose(ps_relT[0:tiles(g), :], rel[:, a, 0:tiles(g)], ident[:]).then_inc(prep_done, 1)

            def spread(g, a, qs):
                T = tiles(g)
                for q in [q for q in qs if q < T // TQ]:
                    if q == 0:
                        pe.wait_ge(relT_ok, g + 1)
                    wait(pe, comb_ok, g * NQ + q - 1)
                    pe.sem_inc(turn, 1)
                    for t in range(q * TQ, (q + 1) * TQ):
                        last = nc.tensor.matmul(ps_row[(q + a) % 2][:, (t % TQ) * P:(t % TQ + 1) * P], sel[0:T, t, :], relT[0:T, :], start=True, stop=True)
                    last.then_inc(row_done, 1)

            prepare(0, 0)
            for qs in ([0, 1], [2, 3], [4]):
                spread(0, 0, qs)
            prepare(1, 1)

            def zmm(g, a, q):
                if q == 0:
                    pe.wait_ge(efT_ok, g + 1)
                    pe.wait_ge(win_ld[a], per(a, g, 16))
                wait(pe, z_ok, g * NQ + q - 1)
                pe.wait_ge(comb_ok, g * NQ + q + 1)
                for t in range(q * TQ, (q + 1) * TQ):
                    last = nc.tensor.matmul(ps_z[(q + a) % 2][:, (t % TQ) * H2:(t % TQ + 1) * H2], comb[:, a, t * P:(t + 1) * P], q_win[:, a, :],
                                            start=True, stop=True)
                last.then_inc(z_done, 1)

            def sums(g, a, t0, t1):
                T = tiles(g)
                for t in range(t0, min(t1, T)):
                    last = nc.tensor.matmul(ps_part[0:U1, 0:WIN], v[:, t, :], hot[:, a, t * WIN:(t + 1) * WIN], start=(t == 0), stop=(t == T - 1))
                    if t == T - 1:
                        last.then_inc(part_done, 1)

            def group(g, a, units=False):
                nxt, nxt2 = following(g)
                if nxt is not None:
                    if nxt2 is None:
                        pe.wait_ge(bad_ok, 1)
                        nc.tensor.transpose(ps_small[0:1, P:2 * P], bad[:, 2:3], ident[:]).then_inc(badT_done, 1)
                    spread(nxt, 1 - a, [2])
                    zmm(g, a, 4)
                    spread(nxt, 1 - a, [3])
                    zmm(nxt, 1 - a, 0)
                    spread(nxt, 1 - a, [4])
                    zmm(nxt, 1 - a, 1)
                    if units:
                        pe.wait_ge(comb_ok, g * NQ + NQ + 4)
                        nc.tensor.matmul(ps_row[a][0:U, :], wu1h[:], hT[:, bass.ds(g * NBT * P, NBT * P)], start=True, stop=True).then_inc(uh_done, 1)
                pe.wait_ge(pmax_ok, g + 1)
                nc.tensor.transpose(ps_small[0:1, 0:P], pmax[:], ident[:]).then_inc(maxT_done, 1)
                pe.wait_ge(gmax_ok, g + 1)
                nc.tensor.matmul(ps_small[:, 0:1], ones[0:1, :], gmax[:], start=True, stop=True).then_inc(maxB_done, 1)
                if nxt2 is not None:
                    prepare(nxt2, a)
                if nxt is not None:
                    zmm(nxt, 1 - a, 2)
                if units:
                    pe.wait_ge(uh_ok, g + 1)
                if nxt2 is not None:
                    spread(nxt2, a, [0, 1])
                pe.wait_ge(v_ok, g + 1)
                pe.wait_ge(hot_ok, 2 * g + 2)
                wait(pe, acc_ok, g)
                sums(g, a, 0, TG // 2)
                if nxt is not None and tiles(nxt) > 3 * TQ:
                    zmm(nxt, 1 - a, 3)
                sums(g, a, TG // 2, TG)
            zmm(0, 0, 0)
            zmm(0, 0, 1)
            spread(1, 1, [0, 1])
            zmm(0, 0, 2)
            zmm(0, 0, 3)
            groups(pe, group, early=lambda g, a: group(g, a, units=True))

            pe.wait_ge(flag_ok, 1)
            misfit = pe.value_load(flag[0:1, 0:1], min_val=0, max_val=1)
            with pe.If(misfit == 1):
                def group_any(g):
                    pe.wait_ge(g_ld, (g + 1) * 48)
                    pe.sem_inc(turn, 1)
                    T = tiles(g)
                    transpose_ef(0, T).then_inc(g_prep, 1)
                    pe.wait_ge(g_efT, g + 1)
                    for q in range(T // TQ):
                        wait(pe, g_zok, g * NQ + q - 1)
                        pe.sem_inc(turn, 1)
                        for t in range(q * TQ, (q + 1) * TQ):
                            last = nc.tensor.matmul(ps_z[q % 2][:, (t % TQ) * H2:(t % TQ + 1) * H2], comb[WIN:P, 0, t * P:(t + 1) * P], q_win[WIN:P, 0, :],
                                                    start=True, stop=True)
                        last.then_inc(g_z, 1)
                    pe.wait_ge(g_pmax, g + 1)
                    nc.tensor.transpose(ps_small[0:1, 0:P], pmax[:], ident[:]).then_inc(g_maxT, 1)
                    pe.wait_ge(g_gmax, g + 1)
                    nc.tensor.matmul(ps_small[:, 0:1], ones[0:1, :], gmax[:], start=True, stop=True).then_inc(g_maxB, 1)
                    pe.wait_ge(g_v, g + 1)

                    def tile_sums(i):
                        pe.wait_ge(g_hot, i + 1)
                        for t in range(T):
                            last = nc.tensor.matmul(ps_part[0:U1, 0:P], v[:, t, :], hot_g[:, t, :], start=(t == 0), stop=(t == T - 1))
                        last.then_inc(g_part, 1)
                    pe.sem_inc(turn, 1)
                    with pe.Fori(0, NT) as i:
                        tile_sums(g * NT + i)
                group_any(0)
                with pe.Fori(1, LAST) as g:
                    group_any(g)
                group_any(LAST)

            pe.wait_ge(sums_ok, 1)
            nc.tensor.matmul(ps_small[:, 0:1], ones[:], zp[:], start=True, stop=True).then_inc(zall_done, 1)
            pe.wait_ge(scale_ok, 1)

            def aggregate(b, a, nt):
                pe.wait_ge(scaled_ok, b + 1)
                wait(pe, u_ok, b - 1)
                nc.tensor.matmul(ps_u[a][0:U, 0:nt * P], wws[:], acc[:, bass.ds(b * NBT * P, nt * P)], start=True, stop=True).then_inc(u_done, 1)

            def update(b, a, nt):
                if nodes_of(b, 2):
                    aggregate(b + 2, a, nodes_of(b, 2))
                pe.wait_ge(su_ok, b + 1)
                wait(pe, y_ok, b - 1)
                for t in range(nt):
                    last = nc.tensor.matmul(ps_y[a][:, t * D:(t + 1) * D], su[:, a, t * P:(t + 1) * P], wu2e[:], start=True, stop=True)
                last.then_inc(y_done, 1)
            aggregate(0, 0, NBT)
            aggregate(1, 1, NBT)
            batches(pe, update)

        @block.vector
        def _(dve):
            steps = [0]

            def chain(ins):
                steps[0] += 1
                ins.then_inc(dve_step, 1)
                dve.wait_ge(dve_step, steps[0])

            for h, (t0, t1) in enumerate(PIECES):
                ts, big = slice(t0, t1), [P, t1 - t0, D]
                dve.wait_ge(x_ld[h], 32 if t1 == NT else 16)
                chain(nc.vector.tensor_reduce(stat[:, 0, ts], x_sb[:, ts, :], AX.X, ALU.add))
                chain(nc.vector.tensor_scalar(stat[:, 1, ts], stat[:, 0, ts], 1.0 / D, None, ALU.mult))
                nc.vector.tensor_tensor(xc[:, ts, :], x_sb[:, ts, :], stat[:, 1, ts].unsqueeze(2).broadcast_to(big), ALU.subtract).then_inc(xc_ok, 1)
            for h, (t0, t1) in enumerate(PIECES):
                ts = slice(t0, t1)
                dve.wait_ge(sq_ok, h + 1)
                chain(nc.vector.tensor_reduce(stat[:, 2, ts], sq[:, ts, :], AX.X, ALU.add))
                nc.vector.tensor_scalar(stat[:, 0, ts], stat[:, 2, ts], 1.0 / D, EPS, ALU.mult, ALU.add).then_inc(var_ok, 1)
            dve.wait_ge(std_ok, 1)
            var, std, inv, t1, t2 = (stat[:, i, :] for i in (0, 3, 4, 1, 2))
            chain(nc.vector.reciprocal(inv, std))
            chain(nc.vector.tensor_tensor(t1, var, inv, ALU.mult))
            chain(nc.vector.tensor_tensor(t2, t1, inv, ALU.mult))
            chain(nc.vector.tensor_scalar(t1, t2, -0.5, 1.5, ALU.mult, ALU.add))
            nc.vector.tensor_tensor(stat[:, 5, :], inv, t1, ALU.mult).then_inc(rstd_ok, 1)

            def normalise(b, a, nt):
                wait(dve, hT_done, b - 1)
                ts = bass.ds(b * NBT, nt)
                nc.vector.tensor_tensor(hn[:, a, 0:nt, :], xc[:, ts, :], stat[:, 5, ts].unsqueeze(2).broadcast_to([P, nt, D]), ALU.mult).then_inc(hn_ok, 1)

            def node_rows(b, a, nt):
                if nodes_of(b, 2):
                    normalise(b + 2, a, nodes_of(b, 2))
                dve.wait_ge(p_done, b + 1)
                wait(dve, p_st[a], 8 * (b - a))
                for j in range(min(2, nt)):
                    last = nc.vector.tensor_copy(pr[:, a, j:nt:2, :], ps_p[a][j][:, 0:-(-nt // 2) * H2].rearrange("p (k u) -> p k u", u=H2))
                last.then_inc(p_ok, 1)
            dve.wait_ge(rstd_ok, 1)
            normalise(0, 0, NBT)
            normalise(1, 1, NBT)
            batches(dve, node_rows)
            dve.wait_ge(first_ld, 32)
            chain(nc.vector.tensor_copy(first_f[:], first_i[:]))
            chain(nc.vector.tensor_scalar(base_f[:], first_f[:], float(N - WIN), None, ALU.min))
            nc.vector.tensor_copy(base_i[:], base_f[:]).then_inc(base_ok, 1)
            chain(nc.vector.tensor_tensor(back[:, 0:LAST], base_f[:, 0:LAST], base_f[:, 1:NG], ALU.subtract))
            chain(nc.vector.tensor_reduce(bad1[:, 0:1], back[:, 0:LAST], AX.X, ALU.max))
            dve.wait_ge(ident_ok, 1)
            nc.vector.tensor_copy(sel[:], ident[0:TG, 0:TG].unsqueeze(2).broadcast_to([TG, TG, P])).then_inc(sel_ok, 1)
            dve.wait_ge(baseB_done, 1)
            nc.vector.tensor_copy(base[:], ps_small[:, 0:NG]).then_inc(baseB_ok, 1)

            def q_rows(b, a, nt):
                dve.wait_ge(q_done, b + 1)
                wait(dve, q_st[a], 8 * (b - a))
                nc.vector.tensor_copy(qr[:, a, 0:nt, :], ps_q[a][:, 0:nt * H2]).then_inc(q_ok, 1)
            batches(dve, q_rows)
            dve.wait_ge(w_ld2, WS)
            nc.vector.tensor_scalar(wa2h[:], wa2[:], 0.5, None, ALU.mult).then_inc(halved, 1)
            nc.vector.tensor_scalar(w2e[0:U, :], w2e[0:U, :], 0.5, None, ALU.mult).then_inc(halved, 1)
            nc.vector.tensor_scalar(wu2e[0:U, :], wu2e[0:U, :], 0.5, None, ALU.mult).then_inc(halved, 1)
            dve.wait_ge(halved, 3)
            dve.wait_ge(ww_done, 1)
            nc.vector.tensor_copy(w2T[:], ps_ww[0:U, 0:U1]).then_inc(ww_ok, 1)
            dve.wait_ge(ww_done, 2)
            nc.vector.tensor_copy(ww[:], ps_ww[0:U1, 0:U]).then_inc(ww_ok, 1)
            nc.vector.memset(zp[:], 0.0)
            dve.wait_ge(const_ok, 8)
            dve.wait_ge(baseB_ok, 1)

            def window(g, a):
                dve.wait_ge(ld[a], per(a, g, 32))
                T = tiles(g)
                nc.vector.tensor_scalar(rel[:, a, 0:T], dst_i[:, a, 0:T], base[:, bass.ds(g, 1)], None, ALU.subtract).then_inc(rel_ok, 1)
                dve.wait_ge(rel_ok, g + 1)
                nc.vector.tensor_reduce(rel_hi[:, bass.ds(g, 1)], rel[:, a, 0:T], AX.X, ALU.max).then_inc(ext_ok, 1)
                nc.vector.tensor_reduce(rel_lo[:, bass.ds(g, 1)], rel[:, a, 0:T], AX.X, ALU.min).then_inc(ext_ok, 1)

            def one_hots(g, a, k):
                T = tiles(g)
                t0, n = k * (T // 2), T // 2
                nc.vector.tensor_tensor(hot[:, a, t0 * WIN:(t0 + n) * WIN].rearrange("p (t n) -> p t n", t=n),
                                        iota[:, 0:WIN].unsqueeze(1).broadcast_to([P, n, WIN]),
                                        rel[:, a, t0:t0 + n].unsqueeze(2).broadcast_to([P, n, WIN]), ALU.is_equal).then_inc(hot_ok, 1)

            def add_part(g, a):
                node = dve.value_load(base_i[0:1, bass.ds(g, 1)], min_val=0, max_val=N - WIN)
                dve.wait_ge(part_done, g + 1)
                win = acc[:, bass.ds(node, WIN)]
                nc.vector.scalar_tensor_tensor(win, win, fade[0:U1, a:a + 1], ps_part[0:U1, 0:WIN], ALU.mult, ALU.add).then_inc(acc_ok, 1)
                nc.vector.tensor_scalar(ref[:, bass.ds(node, WIN)], ones[0:U1, 0:WIN], neg_max[0:U1, bass.ds(g, 1)], -1.0, ALU.mult, ALU.mult).then_inc(ref_ok, 1)
                nc.vector.scalar_tensor_tensor(zp[:], zp[:], fade[:, a:a + 1], wsum[:, a:a + 1], ALU.mult, ALU.add).then_inc(ref_ok, 1)

            def silu_logits(q, th_sem, th_count, s_sem, base_count):
                dve.wait_ge(th_sem, th_count)
                nc.vector.scalar_tensor_tensor(parts(s2, q), parts(th, q), 1.0, parts(z, q), ALU.add, ALU.mult).then_inc(s_sem, 1)
                dve.wait_ge(s_sem, base_count + 1)
                nc.vector.tensor_tensor(parts(z, q)[:, :, U:H2], parts(s2, q)[:, :, U:H2], wa2h[:].unsqueeze(1).broadcast_to([P, TQ, U]), ALU.mult).then_inc(s_sem, 1)
                dve.wait_ge(s_sem, base_count + 2)
                nc.vector.tensor_reduce(lg[:, q * TQ:(q + 1) * TQ], parts(z, q)[:, :, U:H2], AX.X, ALU.add).then_inc(s_sem, 1)

            def weigh(ws, T, a):
                nc.vector.tensor_reduce(wsum[:, a:a + 1], ws[:, 0:T], AX.X, ALU.add)
                nc.vector.tensor_copy(v[:, 0:T, U:U1], ws[:, 0:T].unsqueeze(2))
                return nc.vector.tensor_tensor(v[:, 0:T, 0:U], s2[:, 0:T, 0:U], ws[:, 0:T].unsqueeze(2).broadcast_to([P, T, U]), ALU.mult)

            window(0, 0)
            window(1, 1)
            one_hots(0, 0, 0)
            one_hots(0, 0, 1)
            dve.wait_ge(low_ok, 2)

            def add_rows(g, a, q):
                dve.wait_ge(z_done, g * NQ + q + 1)
                dve.wait_ge(gath[a][q], per(a, g, 16 * TQ))
                nc.vector.tensor_tensor(parts(z, q), ps_z[(q + a) % 2][:].rearrange("p (t u) -> p t u", t=TQ),
                                        p_rows[:, a, q * 512:(q + 1) * 512].rearrange("p (t u) -> p t u", t=TQ), ALU.add).then_inc(z_ok, 1)

            def group(g, a):
                nxt, nxt2 = following(g)
                first = isinstance(g, int) and g == 0
                T = tiles(g)
                for q in range(T // TQ):
                    if q + 1 < T // TQ:
                        add_rows(g, a, q + 1)
                    if q == (2 if nxt2 is not None else 0):
                        if nxt2 is not None:
                            window(nxt2, a)
                        elif nxt is not None:
                            dve.wait_ge(ext_ok, 2 * NG)
                            chain(nc.vector.tensor_reduce(bad[:, 0:1], rel_hi[:], AX.X, ALU.max))
                            chain(nc.vector.tensor_reduce(bad[:, 1:2], rel_lo[:], AX.X, ALU.min))
                            chain(nc.vector.tensor_scalar(bad[:, 0:1], bad[:, 0:1], float(1 - WIN), None, ALU.add))
                            nc.vector.scalar_tensor_tensor(bad[:, 2:3], bad[:, 1:2], -1.0, bad[:, 0:1], ALU.mult, ALU.max).then_inc(bad_ok, 1)
                    if q == 0:
                        wait(dve, v_ok, g)
                    silu_logits(q, th_ok, g * NQ + q + 1, s_ok, (g * NQ + q) * 3)
                    if q == 1 and not first:
                        add_part(g - 1, 1 - a)
                    if q == NQ - 1 and nxt is not None and nxt2 is None:
                        dve.wait_ge(badT_done, 1)
                        chain(nc.vector.tensor_reduce(bad1[:, 1:2], ps_small[0:1, P:2 * P], AX.X, ALU.max))
                        chain(nc.vector.tensor_tensor(bad1[:, 2:3], bad1[:, 1:2], bad1[:, 0:1], ALU.max))
                        nc.vector.tensor_scalar(flag[:], bad1[:, 2:3], 0.0, None, ALU.is_gt).then_inc(flag_ok, 1)
                dve.wait_ge(s_ok, (g * NQ + T // TQ) * 3)
                nc.vector.tensor_scalar(lgb[:, 0:T], lg[:, 0:T], ba2c[:], None, ALU.add).then_inc(lg_ok, 1)
                dve.wait_ge(lg_ok, g + 1)
                nc.vector.tensor_reduce(pmax[:], lgb[:, 0:T], AX.X, ALU.max).then_inc(pmax_ok, 1)
                if nxt is not None:
                    one_hots(nxt, 1 - a, 0)
                dve.wait_ge(maxT_done, g + 1)
                nc.vector.tensor_reduce(gmax[:], ps_small[0:1, 0:P], AX.X, ALU.max).then_inc(gmax_ok, 1)
                if nxt is not None:
                    add_rows(nxt, 1 - a, 0)
                dve.wait_ge(maxB_done, g + 1)
                nm = neg_max[:, bass.ds(g, 1)]
                if first:
                    nc.vector.tensor_scalar(nm, ps_small[:, 0:1], -1.0, None, ALU.mult).then_inc(negm_ok, 1)
                else:
                    nc.vector.scalar_tensor_tensor(nm, ps_small[:, 0:1], -1.0, neg_max[:, bass.ds(g - 1, 1)], ALU.mult, ALU.min).then_inc(negm_ok, 1)
                if nxt is not None:
                    one_hots(nxt, 1 - a, 1)
                dve.wait_ge(w_ok, 2 * g + 2)
                ws = w
                if nxt is None:
                    nc.vector.tensor_tensor(wm[:, 0:T], w[:, 0:T], mask[:], ALU.mult).then_inc(wm_ok, 1)
                    dve.wait_ge(wm_ok, 1)
                    ws = wm
                weigh(ws, T, a).then_inc(v_ok, 1)
            add_rows(0, 0, 0)
            groups(dve, group)
            add_part(LAST, 0)
            dve.wait_ge(ref_ok, 2 * NG)
            nc.vector.tensor_copy(last_neg[:], neg_max[:, LAST:NG]).then_inc(low_ok, 1)

            misfit = dve.value_load(flag[0:1, 0:1], min_val=0, max_val=1)
            with dve.If(misfit == 1):
                nc.vector.memset(acc[:], 0.0).then_inc(g_acc0, 1)
                nc.vector.memset(ref[:], 0.0).then_inc(g_acc0, 1)
                nc.vector.memset(neg_max[:, 0:1], -LOW).then_inc(g_acc0, 1)
                nc.vector.memset(zp[:], 0.0).then_inc(g_acc0, 1)
                dve.wait_ge(g_acc0, 4)
                dve.wait_ge(g_step, 1)

                def group_any(g):
                    nc.vector.memset(bad[:, 0:1], 0.0).then_inc(g_start, 1)
                    k = [0]
                    per_group = NQ + 6
                    T = tiles(g)

                    def link(ins):
                        k[0] += 1
                        ins.then_inc(g_dve, 1)
                        dve.wait_ge(g_dve, g * per_group + k[0])
                    dve.wait_ge(g_gath, g * 32 * TG + 32 * T)
                    for q in range(T // TQ):
                        rows = p_rows[:, :, q * 512:(q + 1) * 512].rearrange("p a (t u) -> p a t u", t=TQ)
                        dve.wait_ge(g_z, g * NQ + q + 1)
                        link(nc.vector.tensor_tensor(parts(s2, q), ps_z[q % 2][:].rearrange("p (t u) -> p t u", t=TQ), rows[:, 0], ALU.add))
                        nc.vector.tensor_tensor(parts(z, q), parts(s2, q), rows[:, 1], ALU.add).then_inc(g_zok, 1)
                        silu_logits(q, g_th, g * NQ + q + 1, g_silu, (g * NQ + q) * 3)
                    dve.wait_ge(g_silu, (g * NQ + T // TQ) * 3)
                    link(nc.vector.tensor_scalar(lgb[:, 0:T], lg[:, 0:T], ba2c[:], None, ALU.add))
                    nc.vector.tensor_reduce(pmax[:], lgb[:, 0:T], AX.X, ALU.max).then_inc(g_pmax, 1)
                    dve.wait_ge(g_maxT, g + 1)
                    nc.vector.tensor_reduce(gmax[:], ps_small[0:1, 0:P], AX.X, ALU.max).then_inc(g_gmax, 1)
                    dve.wait_ge(g_maxB, g + 1)
                    nc.vector.scalar_tensor_tensor(neg_max[:, 1:2], ps_small[:, 0:1], -1.0, neg_max[:, 0:1], ALU.mult, ALU.min).then_inc(g_negm, 1)
                    dve.wait_ge(g_w, 2 * g + 2)
                    link(nc.vector.tensor_copy(neg_max[:, 0:1], neg_max[:, 1:2]))
                    ws = w
                    if is_last(g):
                        link(nc.vector.tensor_tensor(wm[:, 0:T], w[:, 0:T], mask[:], ALU.mult))
                        ws = wm
                    weigh(ws, T, 0).then_inc(g_v, 1)
                    dve.wait_ge(g_v, g + 1)
                    link(nc.vector.scalar_tensor_tensor(zp[:], zp[:], fade[:, 0:1], wsum[:, 0:1], ALU.mult, ALU.add))
                    link(nc.vector.tensor_scalar(acc[:], acc[:], fade[0:U1, 0:1], None, ALU.mult))
                    link(nc.vector.tensor_copy(rel[:, 0, 0:T], dst_i[:, 0, 0:T]))
                    if not is_last(g):
                        link(nc.vector.memset(bad[:, 1:2], 0.0))
                        assert k[0] == per_group

                    def tile_sums(i, count):
                        nc.vector.tensor_scalar(rel[:, 1, 0:T], rel[:, 0, 0:T], tile0[:, bass.ds(i, 1)], None, ALU.subtract).then_inc(g_rel, 1)
                        dve.wait_ge(g_rel, count + 1)
                        nc.vector.tensor_tensor(hot_g[:, 0:T, :], iota[:].unsqueeze(1).broadcast_to([P, T, P]),
                                                rel[:, 1, 0:T].unsqueeze(2).broadcast_to([P, T, P]), ALU.is_equal).then_inc(g_hot, 1)
                        dve.wait_ge(g_part, count + 1)
                        cols = acc[:, bass.ds(i * P, P)]
                        nc.vector.tensor_tensor(cols, cols, ps_part[0:U1, 0:P], ALU.add).then_inc(g_acc, 1)
                        dve.wait_ge(g_acc, count + 1)
                    dve.sem_inc(turn, 1)
                    with dve.Fori(0, NT) as i:
                        tile_sums(i, g * NT + i)
                group_any(0)
                with dve.Fori(1, LAST) as g:
                    group_any(g)
                group_any(LAST)
                nc.vector.tensor_scalar(ref[:], ref[:], neg_max[0:U1, 0:1], None, ALU.subtract).then_inc(g_acc0, 1)
                nc.vector.tensor_copy(last_neg[:], neg_max[:, 0:1]).then_inc(g_acc0, 1)
                dve.wait_ge(g_acc0, 6)
            dve.wait_ge(low_ok, 3)
            dve.sem_inc(sums_ok, 1)
            dve.wait_ge(zall_done, 1)
            nc.vector.tensor_copy(zall[:], ps_small[:, 0:1]).then_inc(zall_ok, 1)
            dve.wait_ge(zall_ok, 1)
            nc.vector.reciprocal(rz[:], zall[:]).then_inc(rz_ok, 1)
            dve.wait_ge(rz_ok, 1)
            nc.vector.tensor_scalar(wws[:], ww[:], rz[0:U1, :], None, ALU.mult).then_inc(scale_ok, 1)

            def rescale(b, a, nt):
                dve.wait_ge(refx_ok, b + 1)
                c = bass.ds(b * NBT * P, nt * P)
                nc.vector.tensor_tensor(acc[:, c], acc[:, c], ref[:, c], ALU.mult).then_inc(scaled_ok, 1)

            def whole_u(b, a, nt):
                dve.wait_ge(u_done, b + 1)
                c = bass.ds(b * NBT * P, nt * P)
                nc.vector.tensor_tensor(hT[0:U, c], hT[0:U, c], ps_u[a][0:U, 0:nt * P], ALU.add).then_inc(u_ok, 1)

            def whole_y(b, a, nt):
                dve.wait_ge(y_done, b + 1)
                wait(dve, out_st[a], 8 * (b - a))
                nc.vector.tensor_tensor(y[:, a, 0:nt, :], ps_y[a][:, 0:nt * D].rearrange("p (t d) -> p t d", t=nt),
                                        x_sb[:, bass.ds(b * NBT, nt), :], ALU.add).then_inc(y_ok, 1)

            def update(b, a, nt):
                if nodes_of(b, 2):
                    rescale(b + 2, a, nodes_of(b, 2))
                if nodes_of(b, 1):
                    whole_u(b + 1, 1 - a, nodes_of(b, 1))
                dve.wait_ge(thu_ok, b + 1)
                wait(dve, y_done, b - 1)
                nc.vector.scalar_tensor_tensor(su[0:U, a, 0:nt * P], thu[:, a, 0:nt * P], 1.0, hT[0:U, bass.ds(b * NBT * P, nt * P)],
                                               ALU.add, ALU.mult).then_inc(su_ok, 1)
                if not (isinstance(b, int) and b == 0):
                    whole_y(b - 1, 1 - a, NBT)
            rescale(0, 0, NBT)
            rescale(1, 1, NBT)
            whole_u(0, 0, NBT)
            batches(dve, update)
            whole_y(NB, 0, 1)
_INS = ["x", "src", "dst", "edge_attr_32"] + ["L0_gnn_" + n for n in
        ("W1", "b1", "W2", "b2", "Wa1", "ba1", "Wa2", "ba2", "Wu1", "bu1", "Wu2", "bu2")]


def kernel(**inputs):
    import numpy as np
    import concourse.bacc as bacc
    from concourse.bass_utils import run_bass_kernel_spmd

    nc = bacc.Bacc("TRN2", target_bir_lowering=False, num_devices=1)
    arrays, args = {}, []
    for name in _INS:
        a = np.ascontiguousarray(inputs[name])
        arrays[name] = a
        args.append(nc.dram_tensor(name, a.shape, mybir.dt.from_np(a.dtype), kind="ExternalInput").ap())
    args.append(nc.dram_tensor("out", inputs["x"].shape, F32, kind="ExternalOutput").ap())
    build(nc, *args)
    r = run_bass_kernel_spmd(nc, [arrays], core_ids=[0])
    return r.results[0]["out"]
```
